# Optimizing a Trainium2 kernel written in Bass

```python
import numpy as np
import jax
import jax.numpy as jnp

def _softmax(x, axis=-1):
    return jax.nn.softmax(x, axis=axis)
def _gelu(x):
    return jax.nn.gelu(x, approximate=True)
def _silu(x):
    return jax.nn.silu(x)
def _sigmoid(x):
    return jax.nn.sigmoid(x)
def _layernorm(x, axis=-1, eps=1e-5):
    m = jnp.mean(x, axis=axis, keepdims=True)
    v = jnp.var(x, axis=axis, keepdims=True)
    return (x - m) / jnp.sqrt(v + eps)
def _scatter_add(tgt, idx, src, axis=0):
    return tgt.at[idx].add(src)
def _segment_sum(src, seg, n):
    return jax.ops.segment_sum(src, seg, n)

kernel_name = 'mk_adj_preln_d2_adj_512_ac8174'

def setup_inputs(seed: int = 0):
    np.random.seed(seed)
    _w = jnp.asarray
    def _rec_inputs():
        import jax
        import jax.numpy as jnp
        _gk = jax.random.key(seed)
        x = -0.0002928 + 1 * jax.random.normal(jax.random.fold_in(_gk, 1), (3327, 512), jnp.float32)
        _a = jax.random.bernoulli(jax.random.fold_in(_gk, 2), 0.00961827, (3327, 3327))
        _a = jnp.logical_or(_a, jnp.eye(3327, dtype=bool))
        _af = _a.astype(jnp.float32)
        adj = _af
        return x, adj
    x, adj = _rec_inputs()
    def _L0_gnn_setup():
        import jax, jax.numpy as jnp
        import numpy as np
        N = 8192
        F_IN = 512
        F_OUT = 512
        DENSITY = 0.01
        key = jax.random.key(seed)
        k_x, k_adj, k_w, k_b = jax.random.split(key, 4)
        input_features = jax.random.normal(k_x, (N, F_IN), dtype=jnp.float32)
        adj = (jax.random.uniform(k_adj, (N, N)) < DENSITY).astype(jnp.float32)
        idx = jnp.arange(N)
        adj = adj.at[idx, idx].set(1.0)
        W = jax.random.normal(k_w, (F_IN, F_OUT), dtype=jnp.float32) / np.sqrt(F_IN)
        b = jax.random.normal(k_b, (F_OUT,), dtype=jnp.float32) * 0.01
        return {'input_features': input_features, 'adj': adj, 'W': W, 'b': b}
    _L0_gnn_all = _L0_gnn_setup()
    _L0_gnn_in = {k: v for k, v in _L0_gnn_all.items() if k in ('W', 'b', )}
    del _L0_gnn_all

    def _L1_gnn_setup():
        import jax, jax.numpy as jnp
        import numpy as np
        N_HEADS = 4
        N_HIDDEN = 512
        SLOPE = 0.01
        NEG = -1000000000.0
        key = jax.random.key(seed)
        k1, k2, k3, k4 = jax.random.split(key, 4)
        N, F_IN = (8192, 512)
        h = jax.random.normal(k1, (N, F_IN), dtype=jnp.float32)
        W = jax.random.normal(k2, (F_IN, N_HIDDEN * N_HEADS), dtype=jnp.float32) * 0.05
        a = jax.random.normal(k3, (N_HEADS, 2 * N_HIDDEN, 1), dtype=jnp.float32) * 0.05
        adj_mat = jnp.where(jax.random.uniform(k4, (N, N)) < 0.01, 0.0, NEG).astype(jnp.float32)
        return {'h': h, 'adj_mat': adj_mat, 'W': W, 'a': a}
    _L1_gnn_all = _L1_gnn_setup()
    _L1_gnn_in = {k: v for k, v in _L1_gnn_all.items() if k in ('W', 'a', )}
    del _L1_gnn_all

    return {
        "x": x,
        "adj": adj,
        "L0_gnn_W": _L0_gnn_in["W"],
        "L0_gnn_b": _L0_gnn_in["b"],
        "L1_gnn_W": _L1_gnn_in["W"],
        "L1_gnn_a": _L1_gnn_in["a"],
    }

def reference(x, adj, L0_gnn_W, L0_gnn_b, L1_gnn_W, L1_gnn_a):
    import jax
    import jax.numpy as jnp
    def _L0_gnn_ref(input_features, adj, W, b):
        import jax, jax.numpy as jnp
        import numpy as np
        N = 8192
        F_IN = 512
        F_OUT = 512
        DENSITY = 0.01
        A = (adj != 0).astype(input_features.dtype)
        hidden = input_features @ W + b
        deg = jnp.sum(A, axis=0)
        return A @ hidden / deg[:, None]

    def _L1_gnn_ref(h, adj_mat, W, a):
        import jax, jax.numpy as jnp
        import numpy as np
        N_HEADS = 4
        N_HIDDEN = 512
        SLOPE = 0.01
        NEG = -1000000000.0
        N = h.shape[0]
        ht = (h @ W).reshape(N, N_HEADS, N_HIDDEN).transpose(1, 0, 2)
        a_src = a[:, :N_HIDDEN, 0]
        a_dst = a[:, N_HIDDEN:, 0]
        src = jnp.einsum('hnd,hd->hn', ht, a_src)
        dst = jnp.einsum('hnd,hd->hn', ht, a_dst)
        e = jax.nn.leaky_relu(src[:, :, None] + dst[:, None, :], SLOPE) + adj_mat[None]
        att = jax.nn.softmax(e, axis=-1)
        h_prime = jnp.einsum('hij,hjd->hid', att, ht)
        return h_prime.mean(axis=0)

    h = jnp.maximum(_layernorm(x, axis=-1), 0.0)
    x = x + _L0_gnn_ref(h, adj, L0_gnn_W, L0_gnn_b)
    h = jnp.maximum(_layernorm(x, axis=-1), 0.0)
    x = x + _L1_gnn_ref(h, adj, L1_gnn_W, L1_gnn_a)
    return x


_drawn_inputs = setup_inputs


def setup_inputs(seed=0):
    import zlib

    import numpy as np

    out = dict(_drawn_inputs(seed))
    spreads = {}
    factors = {'L0_gnn_b': 6.089, 'L1_gnn_a': 5.031}
    for name, (base, spread) in spreads.items():
        noise = np.random.default_rng([zlib.crc32(name.encode()), seed]).standard_normal(out[name].shape)
        drawn = base * np.exp(spread * noise) if base else spread * noise
        out[name] = jnp.asarray(drawn.astype(out[name].dtype))
    for name, factor in factors.items():
        out[name] = (out[name] * factor).astype(out[name].dtype)
    return out
```

```python
from contextlib import ExitStack

import concourse.bass as bass
from concourse import mybir

F32 = mybir.dt.float32
F16 = mybir.dt.float16
ALU = mybir.AluOpType
ACT = mybir.ActivationFunctionType
AX_X = mybir.AxisListType.X
RMAX = bass.bass_isa.ReduceOp.max

N = 3327
P = 128
NT = (N + P - 1) // P
NP = NT * P
LASTP = N - (NT - 1) * P
D = 512
KT = D // P
H = 4
PAIRS = NT // 2
BW = 512
NB = (NP + BW - 1) // BW
FULL = NP // BW
LASTW = NP - FULL * BW
IT = BW // P
EPS = 1e-5
SLOPE = 0.01
HS = 2.0 ** 11
PS = 2.0 ** 15
ZS = 2.0 ** -27
WS = 2.0 ** 15
COEF = 1.0 / (ZS * HS * WS * H)
TINY = 1e-30
LOWEST = -3.0e38

ADJ_RING = 4
A_RING = 2
T_RING = 3
HL_RING = 3


def width(b):
    return BW if not isinstance(b, int) or b < FULL else LASTW


def ring_loop(eng, total, ring, body):
    for slot in range(ring):
        body(slot, slot, 0)
    with eng.Fori(1, total // ring) as turn:
        for slot in range(ring):
            body(turn * ring + slot, slot, turn)
    for slot in range(total % ring):
        body(total // ring * ring + slot, slot, total // ring)


def slot_uses(total, ring, slot):
    return total // ring + (slot < total % ring)


def gnn_kernel(nc, x, adjT, W0, b0, W1, a1, out):
    x1_dram = nc.dram_tensor("x1_dram", (NP, D), F32, kind="Internal").ap()
    rows_dram = nc.dram_tensor("rows_dram", (2 * H + 1, NP), F32, kind="Internal").ap()
    x_t = x.rearrange("(t p) d -> p t d", p=P)
    x1_t = x1_dram.rearrange("(t p) d -> p t d", p=P)
    adj_t = adjT.rearrange("(t p) i -> p t i", p=P)

    with ExitStack() as ctx:
        def sb(name, size, dt):
            return ctx.enter_context(nc.sbuf_tensor(name, [P, size], dt))

        def sem(name):
            return ctx.enter_context(nc.semaphore(name))

        h_reg = sb("h_reg", 2 * NT * D, F16)
        x_reg = sb("x_reg", NT * BW, F32)
        w_reg = sb("w_reg", 2 * KT * H * D, F16)
        ring_reg = sb("ring_reg", 8 * BW, F32)
        z_reg = sb("z_reg", 2 * KT * BW, F16)
        t_reg = sb("t_reg", 2 * T_RING * BW, F32)
        hl_reg = sb("hl_reg", HL_RING * 4 * BW, F16)
        ao_reg = sb("ao_reg", 8 * BW, F32)
        row_reg = sb("row_reg", BW, F32)

        h16 = h_reg[:].rearrange("p (s t d) -> p s t d", s=2, t=NT)
        xs = x_reg[:].rearrange("p (t d) -> p t d", t=NT)
        e_blk = xs
        w16 = w_reg[:].rearrange("p (s k n) -> p s k n", s=2, k=KT)
        w_raw = [ring_reg[:, 0:H * D], ring_reg[:, H * D:2 * H * D], z_reg[:].bitcast(F32), t_reg[:, 0:H * D]]
        a_bc = ao_reg[:].rearrange("p (r c) -> p r c", r=2 * H)
        ln0_stage = hl_reg[:].bitcast(F32).rearrange("p (s u d) -> p s u d", s=3, u=2)
        adj_ring = ring_reg[:].rearrange("p (s u i) -> p s u i", s=ADJ_RING, u=2)
        a_ring = t_reg[:, 0:2 * BW].bitcast(F16).rearrange("p (s u i) -> p s u i", s=A_RING, u=2)
        w0_sb = t_reg[:, 2 * BW:6 * BW].rearrange("p (k n) -> p k n", k=KT)
        s0t = z_reg[:].bitcast(F32).rearrange("p (k i) -> p k i", k=KT)
        adj_max = ao_reg[:, 0:NP]
        adj_cnt = hl_reg[:, 0:NP]
        b0_bc = row_reg[:]
        x_ring = t_reg[:].rearrange("p (s u d) -> p s u d", s=3, u=2)
        ln1_stage = ring_reg[:].rearrange("p (s u d) -> p s u d", s=4, u=2)
        ht_ring = hl_reg[:].bitcast(F32).rearrange("p (s k i) -> p s k i", s=6, k=KT)
        u_bc = ring_reg[:].rearrange("p (h q i) -> p h q i", h=H, q=2)
        z16 = z_reg[:].rearrange("p (s k i) -> p s k i", s=2, k=KT)
        t_ring = x_ring
        hl_ring = hl_reg[:].rearrange("p (r s u i) -> p r s u i", r=HL_RING, s=2, u=2)
        p_acc = ao_reg[:, 0:4 * BW].rearrange("p (a u i) -> p a u i", a=2, u=2)
        out_acc = ao_reg[:, 4 * BW:8 * BW].rearrange("p (t d) -> p t d", t=IT)
        max_bc = row_reg[:]

        ident = sb("ident", P, F32)
        ones32 = sb("ones32", 1, F32)
        ones16 = sb("ones16", 1, F16)
        valid = sb("valid", NT, F32)
        invalid = sb("invalid", 1, F32)
        junk = hl_reg[:, NP:NP + 2 * BW].rearrange("p (u i) -> p u i", u=2)
        credits = sb("credits", 16, F32)
        ticks = sb("ticks", PAIRS, F32)
        bst = sb("bst", NT * 6, F32)
        mv = sb("mv", NT * 2, F32)
        ve = sb("ve", NT, F32)
        sd = sb("sd", NT, F32)
        y0 = sb("y0", NT, F32)
        y1 = sb("y1", NT, F32)
        rs = sb("rs", NT, F32)
        nb = sb("nb", NT, F32)
        wa = sb("wa", KT * 2 * H, F32)
        wmx = sb("wmx", KT, F32)
        wmx1 = sb("wmx1", 1, F32)
        wmax = sb("wmax", 1, F32)
        wsc = sb("wsc", 1, F32)
        coef0 = sb("coef0", 1, F32)
        degp = sb("degp", NT * NB, F32)
        deg = sb("deg", NT, F32)
        rdeg = sb("rdeg", NT, F32)
        cnt_col = sb("cnt_col", IT, F32)
        sdc = ao_reg[:, NP:NP + NT * 2 * H]
        dmx = sb("dmx", 2 * H, F32)
        dall = sb("dall", 2 * H, F32)
        dn = ao_reg[:, NP + NT * 2 * H:NP + NT * 3 * H]
        vv = sb("vv", 2 * H * NT, F32)
        qq = sb("qq", NT, F32)
        lk = sb("lk", NT, F32)
        rows = sb("rows", (2 * H + 1) * NT, F32)
        rinv = sb("rinv", 2 * IT, F32)
        rcoef = sb("rcoef", IT, F32)

        mv3 = mv[:].rearrange("p (t c) -> p t c", c=2)
        bst3 = bst[:].rearrange("p (t c) -> p t c", c=6)
        wa3 = wa[:].rearrange("p (k r) -> p k r", k=KT)
        degp3 = degp[:].rearrange("p (t b) -> p t b", b=NB)
        sdc3 = sdc.rearrange("p (t r) -> p t r", r=2 * H)
        dn3 = dn.rearrange("p (h t) -> p h t", h=H)
        vv4 = vv[:].rearrange("p (q h t) -> p q h t", q=2, h=H)
        rows3 = rows[:].rearrange("p (r t) -> p r t", t=NT)

        z_ps = ctx.enter_context(nc.psum_tensor("z_ps", [P, KT, 512], F32))
        o_ps = ctx.enter_context(nc.psum_tensor("o_ps", [P, 3, 512], F32))
        c_ps = ctx.enter_context(nc.psum_tensor("c_ps", [P, 512], F32))

        s_var = sem("s_var")
        s_sqrt = sem("s_sqrt")
        s_ln = sem("s_ln")
        dve_step = sem("dve_step")
        steps = [0]

        def link(dve, ins):
            steps[0] += 1
            ins.then_inc(dve_step, 1)
            dve.wait_ge(dve_step, steps[0])

        def ln_scalars(dve, layer):
            nc.vector.tensor_scalar(ve[:], mv3[:, :, 1], EPS, None, ALU.add).then_inc(s_var, 1)
            dve.wait_ge(s_sqrt, layer + 1)
            link(dve, nc.vector.reciprocal(y0[:], sd[:]))
            link(dve, nc.vector.tensor_tensor(y1[:], y0[:], y0[:], ALU.mult))
            link(dve, nc.vector.tensor_tensor(y1[:], y1[:], ve[:], ALU.mult))
            link(dve, nc.vector.tensor_scalar(y1[:], y1[:], -0.5, 1.5, ALU.mult, ALU.add))
            link(dve, nc.vector.scalar_tensor_tensor(out=rs[:], in0=y1[:], scalar=HS, in1=y0[:],
                                                     op0=ALU.mult, op1=ALU.mult))
            nc.vector.scalar_tensor_tensor(out=nb[:], in0=mv3[:, :, 0], scalar=-1.0, in1=rs[:],
                                           op0=ALU.mult, op1=ALU.mult).then_inc(s_ln, 1)

        def ln_sqrt(act, layer):
            act.wait_ge(s_var, layer + 1)
            nc.scalar.activation(sd[:], ve[:], ACT.Sqrt).then_inc(s_sqrt, 1)

        chunks = [(0, 7), (7, 14), (14, 20), (20, NT)]
        x_in = [sem(f"x_in{c}") for c in range(len(chunks))]
        w_in = [sem(f"w_in{k}") for k in range(KT)]
        a_in = sem("a_in")
        s_bst = sem("s_bst")
        s_mv = sem("s_mv")
        s_const = sem("s_const")
        s_ident0 = sem("s_ident0")
        stage_ready = sem("stage_ready")
        hi_done = sem("hi_done")
        stage_free = sem("stage_free")
        s_wmx = sem("s_wmx")
        s_wmax = sem("s_wmax")
        w_scaled = sem("w_scaled")
        w_hi = sem("w_hi")
        s_wred = sem("s_wred")

        with nc.Block() as block:
            @block.sync
            def _(sp):
                for c, (t0, t1) in enumerate(chunks):
                    sp.dma_start(xs[:, t0:t1, :], x_t[:, t0:t1, :]).then_inc(x_in[c], 16)
                sp.dma_start(a_bc, a1.rearrange("h (q c) o -> (h q) (c o)", q=2)
                             .partition_broadcast(P)).then_inc(a_in, 16)
                for k in range(KT):
                    sp.dma_start(w_raw[k], W1[k * P:(k + 1) * P, :]).then_inc(w_in[k], 16)

            @block.gpsimd
            def _(pool):
                nc.gpsimd.memset(ident[:], 0.0).then_inc(s_ident0, 1)
                nc.gpsimd.memset(valid[:], 1.0).then_inc(s_ident0, 1)
                pool.wait_ge(s_ident0, 2)
                nc.gpsimd.affine_select(out=ident[:], in_=ident[:], compare_op=ALU.not_equal, fill=1.0,
                                        base=0, pattern=[[-1, P]], channel_multiplier=1).then_inc(s_const, 1)
                nc.gpsimd.affine_select(out=valid[:, NT - 1:NT], in_=valid[:, NT - 1:NT],
                                        compare_op=ALU.is_ge, fill=0.0, base=LASTP - 1, pattern=[[0, 1]],
                                        channel_multiplier=-1).then_inc(s_const, 1)
                pool.wait_ge(s_wmx, 1)
                nc.gpsimd.partition_all_reduce(wmax[:], wmx1[:], P, RMAX).then_inc(s_wmax, 1)

            @block.scalar
            def _(act):
                ln_sqrt(act, 0)
                act.wait_ge(s_ln, 1)
                with act.Fori(0, PAIRS) as p:
                    act.wait_ge(stage_free, p + 1)
                    for u in range(2):
                        t = p * 2 + u
                        nc.scalar.activation(ln0_stage[:, p % 3, u], xs[:, t], ACT.Relu, bias=nb[:, bass.ds(t, 1)],
                                             scale=rs[:, bass.ds(t, 1)]).then_inc(stage_ready, 1)
                for k in range(KT):
                    act.wait_ge(w_scaled, k + 1)
                    nc.scalar.activation(w16[:, 0, k], w_raw[k], ACT.Copy).then_inc(w_hi, 1)

            @block.vector
            def _(dve):
                nc.vector.memset(ones32[:], 1.0)
                nc.vector.memset(ones16[:], 1.0).then_inc(stage_free, 3)
                for c, (t0, t1) in enumerate(chunks):
                    dve.wait_ge(x_in[c], 16)
                    with dve.Fori(t0, t1) as t:
                        nc.vector.bn_stats(bst3[:, t], xs[:, t]).then_inc(s_bst, 1)
                dve.wait_ge(s_bst, NT)
                for t in range(NT):
                    nc.vector.bn_aggr(mv3[:, t], bst3[:, t]).then_inc(s_mv, 1)
                dve.wait_ge(s_mv, NT)
                ln_scalars(dve, 0)
                with dve.Fori(0, PAIRS) as p:
                    dve.wait_ge(stage_ready, p * 2 + 2)
                    nc.vector.tensor_scalar(h16[:, 0, bass.ds(p * 2, 2)], ln0_stage[:, p % 3], 1.0, None,
                                            ALU.mult).then_inc(hi_done, 1)
                    dve.wait_ge(hi_done, p + 1)
                    nc.vector.tensor_tensor(h16[:, 1, bass.ds(p * 2, 2)], ln0_stage[:, p % 3],
                                            h16[:, 0, bass.ds(p * 2, 2)], ALU.subtract).then_inc(stage_free, 1)
                dve.wait_ge(s_const, 2)
                link(dve, nc.vector.tensor_scalar(invalid[:], valid[:, NT - 1:NT], -1.0, 1.0, ALU.mult, ALU.add))
                for k in range(KT):
                    dve.wait_ge(w_in[k], 16)
                    nc.vector.tensor_reduce(wmx[:, k:k + 1], w_raw[k], AX_X, ALU.max,
                                            apply_absolute_value=True).then_inc(s_wred, 1)
                dve.wait_ge(s_wred, KT)
                nc.vector.tensor_reduce(wmx1[:], wmx[:], AX_X, ALU.max).then_inc(s_wmx, 1)
                dve.wait_ge(a_in, 16)
                for k in range(KT):
                    for r in range(2 * H):
                        h = r // 2
                        link(dve, nc.vector.tensor_tensor_reduce(
                            out=row_reg[:], in0=w_raw[k][:, h * D:(h + 1) * D], in1=a_bc[:, r], scale=1.0,
                            scalar=0.0, op0=ALU.mult, op1=ALU.add, accum_out=wa3[:, k, r:r + 1]))
                dve.wait_ge(s_wmax, 1)
                link(dve, nc.vector.tensor_scalar(wmax[:], wmax[:], TINY, None, ALU.max))
                link(dve, nc.vector.reciprocal(wsc[:], wmax[:]))
                link(dve, nc.vector.tensor_scalar(wsc[:], wsc[:], WS, None, ALU.mult))
                link(dve, nc.vector.tensor_scalar(coef0[:], wmax[:], COEF, None, ALU.mult))
                for k in range(KT):
                    nc.vector.tensor_scalar(w_raw[k], w_raw[k], wsc[:], None, ALU.mult).then_inc(w_scaled, 1)
                for k in range(KT):
                    dve.wait_ge(w_hi, k + 1)
                    link(dve, nc.vector.tensor_tensor(w16[:, 1, k], w_raw[k], w16[:, 0, k], ALU.subtract))

        adj_in = [sem(f"adj_in{s}") for s in range(ADJ_RING)]
        w0_in = sem("w0_in")
        b0_in = sem("b0_in")
        mx_done = sem("mx_done")
        cnt_done = sem("cnt_done")
        a_ready = sem("a_ready")
        a_pe = sem("a_pe")
        a_act = sem("a_act")
        s0_bank = sem("s0_bank")
        s0_out = sem("s0_out")
        cnt_ps = sem("cnt_ps")
        cnt_sb = sem("cnt_sb")
        o0_done = sem("o0_done")
        o0_out = sem("o0_out")
        MX0 = 2 * (ADJ_RING + 1)

        with nc.Block() as block:
            @block.sync
            def _(sp):
                def load(b, p, slot, turn):
                    W = width(b)
                    g = b * PAIRS + p
                    sp.wait_ge(mx_done, MX0 + 2 * (g - back(slot, turn)) + 2)
                    sp.dma_start(adj_ring[:, slot, :, 0:W],
                                 adj_t[:, bass.ds(p * 2, 2), bass.ds(b * BW, W)]).then_inc(adj_in[slot], 16)

                def back(slot, turn):
                    if isinstance(turn, int) and turn == 0:
                        return 1 if slot == 0 else ADJ_RING + 1
                    return ADJ_RING

                def block_loads(b):
                    for slot in range(ADJ_RING):
                        load(b, slot, slot, 0)
                    with sp.Fori(1, PAIRS // ADJ_RING) as turn:
                        for slot in range(ADJ_RING):
                            load(b, turn * ADJ_RING + slot, slot, turn)
                    load(b, PAIRS - 1, 0, PAIRS // ADJ_RING)

                sp.dma_start(w0_sb, W0.rearrange("(k p) n -> p k n", p=P)).then_inc(w0_in, 16)
                sp.dma_start(b0_bc, b0.partition_broadcast(P)).then_inc(b0_in, 16)
                with sp.Fori(0, FULL) as b:
                    block_loads(b)
                block_loads(FULL)

            @block.vector
            def _(dve):
                link(dve, nc.vector.memset(adj_cnt.bitcast(F32), 0.0))
                nc.vector.memset(adj_max, LOWEST).then_inc(mx_done, MX0)

                def pair(b, p, slot, turn):
                    W = width(b)
                    g = b * PAIRS + p
                    cols = bass.ds(b * BW, W)
                    dve.wait_ge(adj_in[slot], (b * slot_uses(PAIRS, ADJ_RING, slot) + turn + 1) * 16)
                    dve.wait_ge(a_pe, g + 1)
                    dve.wait_ge(a_act, g * 2 + 2)
                    for u in range(2):
                        nc.vector.tensor_scalar(a_ring[:, g % A_RING, u, 0:W], adj_ring[:, slot, u, 0:W], 0.0,
                                                valid[:, bass.ds(p * 2 + u, 1)], ALU.not_equal,
                                                ALU.mult).then_inc(a_ready, 1)
                    for u in range(2):
                        dve.wait_ge(mx_done, g * 2 + MX0 + u)
                        nc.vector.tensor_tensor(adj_max[:, cols], adj_max[:, cols], adj_ring[:, slot, u, 0:W],
                                                ALU.max).then_inc(mx_done, 1)
                        dve.wait_ge(a_ready, g * 2 + u + 1)
                        dve.wait_ge(cnt_done, g * 2 + u + 1)
                        nc.vector.tensor_tensor(adj_cnt[:, cols], adj_cnt[:, cols], a_ring[:, g % A_RING, u, 0:W],
                                                ALU.add).then_inc(cnt_done, 1)

                def head(b):
                    for p in range(3):
                        pair(b, p, p, 0)

                def rest(b):
                    pair(b, 3, 3, 0)
                    with dve.Fori(1, PAIRS // ADJ_RING) as turn:
                        for slot in range(ADJ_RING):
                            pair(b, turn * ADJ_RING + slot, slot, turn)
                    pair(b, PAIRS - 1, 0, PAIRS // ADJ_RING)

                def evacuate(b):
                    W = width(b)
                    n = W // P
                    dve.wait_ge(cnt_ps, b + 1)
                    nc.vector.tensor_copy(cnt_col[:, 0:n], c_ps[:, 0:n]).then_inc(cnt_sb, 1)
                    dve.wait_ge(cnt_sb, b + 2)
                    for it in range(n):
                        f = b * IT + it
                        dve.wait_ge(o0_done, f + 2)
                        nc.vector.scalar_tensor_tensor(out=xs[:, f], in0=b0_bc, scalar=cnt_col[:, it:it + 1],
                                                       in1=o_ps[:, it % 2], op0=ALU.mult,
                                                       op1=ALU.add).then_inc(o0_out, 1)

                nc.vector.memset(credits[:, 0:1], 0.0).then_inc(a_pe, A_RING)
                nc.vector.memset(credits[:, 1:2], 0.0).then_inc(a_act, 2 * A_RING)
                nc.vector.memset(credits[:, 2:3], 0.0).then_inc(cnt_done, 1)
                nc.vector.memset(credits[:, 3:4], 0.0).then_inc(cnt_sb, 1)
                nc.vector.memset(credits[:, 4:5], 0.0).then_inc(o0_out, 2)
                nc.vector.memset(credits[:, 5:6], 0.0).then_inc(o0_done, 1)
                dve.wait_ge(b0_in, 16)
                head(0)
                with dve.Fori(0, FULL - 1) as b:
                    rest(b)
                    head(b + 1)
                    evacuate(b)
                for b in (FULL - 1, FULL):
                    rest(b)
                    if b < FULL:
                        head(b + 1)
                    evacuate(b)

            @block.scalar
            def _(act):
                def block_work(b):
                    W = width(b)
                    Wv = W if W == BW else W - (NP - N)
                    with act.Fori(0, PAIRS) as p:
                        g = b * PAIRS + p
                        for u in range(2):
                            act.wait_ge(a_ready, g * 2 + u + 1)
                            act.wait_ge(a_act, g * 2 + u + 2 * A_RING - 1)
                            nc.scalar.activation(junk[:, u, 0:Wv], a_ring[:, g % A_RING, u, 0:Wv], ACT.Copy,
                                                 accum_out=degp3[:, bass.ds(p * 2 + u, 1), b]).then_inc(a_act, 1)
                    act.wait_ge(o0_done, b * IT + 1)
                    for k in range(KT):
                        if k < KT - 1:
                            act.wait_ge(s0_bank, b * (KT - 1) + k + 1)
                        else:
                            act.wait_ge(a_pe, (b + 1) * PAIRS + A_RING)
                        nc.scalar.activation(s0t[:, k, 0:W], z_ps[:, k, 0:W], ACT.Copy,
                                             scale=1.0 / HS).then_inc(s0_out, 1)

                with act.Fori(0, FULL) as b:
                    block_work(b)
                block_work(FULL)

            @block.tensor
            def _(pe):
                def pair(b, p, first=False, last=False, evacuated=None):
                    W = width(b)
                    g = b * PAIRS + p
                    pe.wait_ge(a_ready, g * 2 + 2)
                    for k in range(KT):
                        if evacuated is not None:
                            pe.wait_ge(s0_out, evacuated * KT + k + 1)
                        for u in range(2):
                            for s in range(2):
                                mm = nc.tensor.matmul(
                                    z_ps[:, k, 0:W], h16[:, s, p * 2 + u, k * P:(k + 1) * P],
                                    a_ring[:, g % A_RING, u, 0:W], start=first and u == 0 and s == 0,
                                    stop=last and u == 1 and s == 1)
                        if k == KT - 1:
                            mm.then_inc(a_pe, 1)
                        elif last:
                            mm.then_inc(s0_bank, 1)

                def project(b):
                    W = width(b)
                    n = W // P
                    pe.wait_ge(cnt_done, (b + 1) * NT + 1)
                    pe.wait_ge(cnt_sb, b + 1)
                    for it in range(n):
                        mm = nc.tensor.matmul(c_ps[:, it:it + 1], adj_cnt[:, bass.ds(b * BW + it * P, P)], ones16[:],
                                              start=True, stop=True)
                    mm.then_inc(cnt_ps, 1)
                    pe.wait_ge(s0_out, (b + 1) * KT)
                    for it in range(n):
                        f = b * IT + it
                        pe.wait_ge(o0_out, f + 1)
                        for k in range(KT):
                            mm = nc.tensor.matmul(o_ps[:, it % 2], s0t[:, k, it * P:(it + 1) * P], w0_sb[:, k],
                                                  start=k == 0, stop=k == KT - 1)
                        mm.then_inc(o0_done, 1)

                pe.wait_ge(w0_in, 16)
                pair(0, 0, first=True)
                with pe.Fori(0, FULL - 1) as b:
                    with pe.Fori(1, PAIRS - 1) as p:
                        pair(b, p)
                    pair(b, PAIRS - 1, last=True)
                    pair(b + 1, 0, first=True, evacuated=b)
                    project(b)
                for b in (FULL - 1, FULL):
                    with pe.Fori(1, PAIRS - 1) as p:
                        pair(b, p)
                    pair(b, PAIRS - 1, last=True)
                    if b < FULL:
                        pair(b + 1, 0, first=True, evacuated=b)
                    project(b)

        x_in1 = [sem(f"x_in1_{s}") for s in range(3)]
        x1_ready = sem("x1_ready")
        x1_bst = sem("x1_bst")
        s_mv1 = sem("s_mv1")
        x1_out = sem("x1_out")
        mt_ps = sem("mt_ps")
        mt_red = sem("mt_red")
        st1_ready = sem("st1_ready")
        st1_split = sem("st1_split")
        hi1_done = sem("hi1_done")
        tr_ps = sem("tr_ps")
        tr_sb = sem("tr_sb")
        sd_ps = sem("sd_ps")
        s_dmx = sem("s_dmx")
        s_dall = sem("s_dall")
        s_dn = sem("s_dn")
        s_vv = sem("s_vv")
        s_uarg = sem("s_uarg")
        s_uexp = sem("s_uexp")
        s_rows = sem("s_rows")
        rt_ps = sem("rt_ps")
        rt_sb = sem("rt_sb")
        rows_out = sem("rows_out")
        NR = 2 * H + 1
        RH = NR * NT // 2
        max_groups = [(t, min(t + IT, NT)) for t in range(0, NT, IT)]
        row_stage = row_reg[:, 0:2 * P].rearrange("p (a i) -> p a i", a=2)

        with nc.Block() as block:
            @block.sync
            def _(sp):
                def load(p, slot, turn):
                    if not (isinstance(turn, int) and turn == 0):
                        sp.wait_ge(x1_ready, p * 2 - 4)
                    sp.dma_start(x_ring[:, slot], x_t[:, bass.ds(p * 2, 2), :]).then_inc(x_in1[slot], 16)

                def store(p):
                    sp.wait_ge(x1_ready, p * 2 + 2)
                    sp.dma_start(x1_t[:, bass.ds(p * 2, 2), :], xs[:, bass.ds(p * 2, 2)]).then_inc(x1_out, 16)

                for p in range(3):
                    load(p, p, 0)
                with sp.Fori(1, PAIRS // 3) as turn:
                    for slot in range(3):
                        load(turn * 3 + slot, slot, turn)
                        store(turn * 3 + slot - 3)
                load(PAIRS - 1, 0, PAIRS // 3)
                for p in range(PAIRS - 4, PAIRS):
                    store(p)
                sp.wait_ge(rt_sb, 2)
                rows_v = rows_dram.rearrange("r (t i) -> (r t) i", i=P)
                for a in range(2):
                    sp.dma_start(rows_v[a * RH:(a + 1) * RH, :], row_stage[0:RH, a]).then_inc(rows_out, 16)
                sp.wait_ge(rows_out, 32)
                sp.wait_ge(x1_out, 16 * PAIRS)

            @block.gpsimd
            def _(pool):
                pool.wait_ge(s_dmx, 1)
                nc.gpsimd.partition_all_reduce(dall[:], dmx[:], P, RMAX).then_inc(s_dall, 1)

            @block.scalar
            def _(act):
                ln_sqrt(act, 1)
                act.wait_ge(s_ln, 2)

                def relu(t, slot):
                    nc.scalar.activation(ln1_stage[:, slot, t % 2], xs[:, t], ACT.Relu, bias=nb[:, bass.ds(t, 1)],
                                         scale=rs[:, bass.ds(t, 1)]).then_inc(st1_ready, 1)

                for t in range(NT + 1):
                    if t < NT:
                        p = t // 2
                        if t % 2 == 0 and p >= 4:
                            act.wait_ge(st1_split, p - 3)
                            act.wait_ge(tr_ps, 2 * (p - 3))
                        relu(t, p % 4)
                    if t > 0:
                        act.wait_ge(tr_ps, t)
                        if t > 6:
                            act.wait_ge(sd_ps, t - 6)
                        nc.scalar.activation(ht_ring[:, (t - 1) % 6], o_ps[:, (t - 1) % 3]
                                             .rearrange("p (k i) -> p k i", k=KT), ACT.Copy).then_inc(tr_sb, 1)
                for h in range(H):
                    act.wait_ge(s_dn, h + 1)
                    for q, f in ((0, 1.0), (1, SLOPE)):
                        nc.scalar.activation(vv4[:, q, h], dn3[:, h], ACT.Exp, scale=f).then_inc(s_vv, 1)
                act.wait_ge(s_uarg, 2 * H)
                nc.scalar.activation(rows[:, 0:2 * H * NT], rows[:, 0:2 * H * NT], ACT.Exp).then_inc(s_uexp, 1)
                for a in range(2):
                    act.wait_ge(rt_ps, a + 1)
                    nc.scalar.activation(row_stage[0:RH, a], o_ps[0:RH, a, 0:P], ACT.Copy).then_inc(rt_sb, 1)

            @block.tensor
            def _(pe):
                for n, (t0, t1) in enumerate(max_groups):
                    if n >= KT:
                        pe.wait_ge(mt_red, n - KT + 1)
                    for t in range(t0, t1):
                        mm = nc.tensor.transpose(z_ps[:, n % KT, (t - t0) * P:(t - t0 + 1) * P],
                                                 adj_max[:, t * P:(t + 1) * P], ident[:])
                    mm.then_inc(mt_ps, 1)

                def scores(t):
                    pe.wait_ge(tr_sb, t + 1)
                    for k in range(KT):
                        mm = nc.tensor.matmul(c_ps[:, t * 2 * H:(t + 1) * 2 * H], ht_ring[:, t % 6, k], wa3[:, k],
                                              start=k == 0, stop=k == KT - 1)
                    mm.then_inc(sd_ps, 1)

                for t in range(NT):
                    pe.wait_ge(st1_ready, t + 1)
                    if t >= 3:
                        pe.wait_ge(tr_sb, t - 2)
                    for k in range(KT):
                        mm = nc.tensor.transpose(o_ps[:, t % 3, k * P:(k + 1) * P],
                                                 ln1_stage[:, (t // 2) % 4, t % 2, k * P:(k + 1) * P], ident[:])
                    mm.then_inc(tr_ps, 1)
                    if t >= 1:
                        scores(t - 1)
                scores(NT - 1)
                pe.wait_ge(s_rows, 1)
                pe.wait_ge(tr_sb, NT)
                for a in range(2):
                    nc.tensor.transpose(o_ps[0:RH, a, 0:P], rows[:, a * RH:(a + 1) * RH],
                                        ident[:]).then_inc(rt_ps, 1)

            @block.vector
            def _(dve):
                link(dve, nc.vector.tensor_reduce(deg[:], degp3, AX_X, ALU.add))
                link(dve, nc.vector.tensor_tensor(deg[:, NT - 1:NT], deg[:, NT - 1:NT], invalid[:], ALU.add))
                link(dve, nc.vector.reciprocal(rdeg[:], deg[:]))

                def x1_pair(p, slot, turn):
                    dve.wait_ge(x_in1[slot], (turn + 1) * 16)
                    for u in range(2):
                        t = p * 2 + u
                        nc.vector.scalar_tensor_tensor(out=xs[:, t], in0=xs[:, t], scalar=rdeg[:, bass.ds(t, 1)],
                                                       in1=x_ring[:, slot, u], op0=ALU.mult,
                                                       op1=ALU.add).then_inc(x1_ready, 1)
                    for u in range(2):
                        t = p * 2 + u
                        dve.wait_ge(x1_ready, t + 1)
                        nc.vector.bn_stats(bst3[:, t], xs[:, t]).then_inc(x1_bst, 1)

                ring_loop(dve, PAIRS, 3, x1_pair)
                dve.wait_ge(x1_bst, NT)
                for t in range(NT):
                    nc.vector.bn_aggr(mv3[:, t], bst3[:, t]).then_inc(s_mv1, 1)
                dve.wait_ge(s_mv1, NT)
                ln_scalars(dve, 1)
                for n, (t0, t1) in enumerate(max_groups):
                    dve.wait_ge(mt_ps, n + 1)
                    nc.vector.tensor_reduce(rows3[:, 2 * H, t0:t1],
                                            z_ps[:, n % KT, 0:(t1 - t0) * P].rearrange("p (t i) -> p t i", i=P),
                                            AX_X, ALU.max).then_inc(mt_red, 1)
                with dve.Fori(0, PAIRS) as p:
                    dve.wait_ge(st1_ready, p * 2 + 2)
                    nc.vector.tensor_scalar(h16[:, 0, bass.ds(p * 2, 2)], ln1_stage[:, p % 4], 1.0, None,
                                            ALU.mult).then_inc(hi1_done, 1)
                    dve.wait_ge(hi1_done, p + 1)
                    nc.vector.tensor_tensor(h16[:, 1, bass.ds(p * 2, 2)], ln1_stage[:, p % 4],
                                            h16[:, 0, bass.ds(p * 2, 2)], ALU.subtract).then_inc(st1_split, 1)
                dve.wait_ge(sd_ps, NT)
                link(dve, nc.vector.tensor_scalar(sdc, c_ps[:, 0:NT * 2 * H], 1.0 / HS, None, ALU.mult))
                nc.vector.tensor_reduce(dmx[:], sdc.rearrange("p (t r) -> p r t", r=2 * H), AX_X,
                                        ALU.max).then_inc(s_dmx, 1)
                dve.wait_ge(s_dall, 1)
                for h in range(H):
                    nc.vector.tensor_scalar(dn3[:, h], sdc3[:, :, 2 * h + 1], dall[:, 2 * h + 1:2 * h + 2], None,
                                            ALU.subtract).then_inc(s_dn, 1)
                for h in range(H):
                    link(dve, nc.vector.tensor_scalar(qq[:], sdc3[:, :, 2 * h], dall[:, 2 * h + 1:2 * h + 2], None,
                                                      ALU.add))
                    link(dve, nc.vector.scalar_tensor_tensor(out=lk[:], in0=qq[:], scalar=SLOPE, in1=qq[:],
                                                             op0=ALU.mult, op1=ALU.max))
                    nc.vector.tensor_tensor(rows3[:, 2 * h], qq[:], lk[:], ALU.subtract).then_inc(s_uarg, 1)
                    nc.vector.scalar_tensor_tensor(out=rows3[:, 2 * h + 1], in0=qq[:], scalar=SLOPE, in1=lk[:],
                                                   op0=ALU.mult, op1=ALU.subtract).then_inc(s_uarg, 1)
                    dve.wait_ge(s_uarg, 2 * h + 2)
                dve.wait_ge(s_vv, 2 * H)
                link(dve, nc.vector.tensor_scalar(vv[:].rearrange("p (r t) -> p r t", t=NT)[:, :, NT - 1],
                                                  vv[:].rearrange("p (r t) -> p r t", t=NT)[:, :, NT - 1],
                                                  valid[:, NT - 1:NT], None, ALU.mult))
                dve.wait_ge(s_uexp, 1)
                nc.vector.tensor_scalar(rows[:, 0:2 * H * NT], rows[:, 0:2 * H * NT], PS, None,
                                        ALU.mult).then_inc(s_rows, 1)

        u_in = [sem(f"u_in{h}") for h in range(H)]
        e_in = [sem(f"e_in{p}") for p in range(PAIRS)]
        mb_in = sem("mb_in")
        x1_in = sem("x1_in")
        out_st = sem("out_st")
        e_here = sem("e_here")
        e_sub = sem("e_sub")
        e_ready = sem("e_ready")
        t1_ready = sem("t1_ready")
        stt_done = sem("stt_done")
        p_ready = sem("p_ready")
        acc_done = sem("acc_done")
        hi_ready = sem("hi_ready")
        lo_ready = sem("lo_ready")
        hl_free = sem("hl_free")
        z_bank = sem("z_bank")
        z_hi = sem("z_hi")
        z_lo = sem("z_lo")
        rs_ps = sem("rs_ps")
        rs_sb = sem("rs_sb")
        rinv_done = sem("rinv_done")
        o_done = sem("o_done")
        o_out = sem("o_out")
        LOOP0, LOOP1 = 5, PAIRS - 2
        E_LATE = PAIRS - LOOP1
        assert LOOP1 - LOOP0 + (LOOP1 - LOOP0 + 1) == PAIRS

        def seg_next(b, h):
            return (b, h + 1) if h < H - 1 else ((b + 1, 0) if not isinstance(b, int) or b < FULL else None)

        def o_before(b, h):
            if isinstance(b, int) and b == FULL:
                return FULL * H * IT + h * (LASTW // P)
            return (b * H + h) * IT

        def e_of(b, h, p):
            looped = not isinstance(p, int)
            if h == 0 and isinstance(b, int) and b == 0:
                return (b, p + 1) if looped or p < PAIRS - 1 else None
            if h == 0:
                return (b, p + E_LATE) if looped or p == LOOP0 - 1 else None
            if h == H - 1 and (not isinstance(b, int) or b < FULL):
                return (b + 1, p - LOOP0) if looped else None
            return None

        def blocks(eng, body, first=0):
            for b in range(first):
                body(b)
            with eng.Fori(first, FULL - 1) as b:
                body(b)
            body(FULL - 1)
            body(FULL)

        with nc.Block() as block:
            @block.sync
            def _(sp):
                def load_u(b, h):
                    W = width(b)
                    sp.dma_start(u_bc[:, h, :, 0:W], rows_dram[2 * h:2 * h + 2, bass.ds(b * BW, W)]
                                 .partition_broadcast(P)).then_inc(u_in[h], 16)

                def load_max(b):
                    W = width(b)
                    sp.dma_start(max_bc[:, 0:W], rows_dram[2 * H, bass.ds(b * BW, W)]
                                 .partition_broadcast(P)).then_inc(mb_in, 16)

                def load_e(b, p):
                    W = width(b)
                    sp.dma_start(e_blk[:, bass.ds(p * 2, 2), 0:W],
                                 adj_t[:, bass.ds(p * 2, 2), bass.ds(b * BW, W)]).then_inc(e_in[p], 16)

                def load_x1(b):
                    n = width(b) // P
                    sp.dma_start(out_acc[:, 0:n], x1_t[:, bass.ds(b * IT, n), :]).then_inc(x1_in, 16)

                def store(b):
                    sp.wait_ge(o_out, (b + 1) * H * IT + 2 if not isinstance(b, int) or b < FULL
                               else FULL * H * IT + H * LASTW // P + 2)
                    if isinstance(b, int) and b == FULL:
                        r0 = FULL * BW
                        sp.dma_start(out[r0:r0 + P, :], out_acc[:, 0]).then_inc(out_st, 16)
                        sp.dma_start(out[r0 + P:N, :], out_acc[0:LASTP, 1]).then_inc(out_st, 16)
                    else:
                        sp.dma_start(out[bass.ds(b * BW, BW), :].rearrange("(t p) d -> p t d", p=P),
                                     out_acc[:, 0:IT]).then_inc(out_st, 16)

                load_max(0)
                load_u(0, 0)
                for p in range(PAIRS):
                    load_e(0, p)
                for h in range(1, H):
                    load_u(0, h)
                load_x1(0)

                def body(b):
                    if not isinstance(b, int) or b < FULL:
                        nxt = b + 1
                        for h in range(H - 1):
                            sp.wait_ge(p_ready, (b * H + h + 1) * PAIRS)
                            load_u(nxt, h)
                        sp.wait_ge(e_sub, (b + 1) * NT)
                        load_max(nxt)

                        for p in range(PAIRS):
                            sp.wait_ge(p_ready, (b * H + H - 1) * PAIRS + p + 1)
                            load_e(nxt, p)
                        sp.wait_ge(p_ready, (b + 1) * H * PAIRS)
                        load_u(nxt, H - 1)
                    store(b)
                    if not isinstance(b, int) or b < FULL:
                        sp.wait_ge(out_st, (b + 1) * 16)
                        load_x1(nxt)
                    else:
                        sp.wait_ge(out_st, (FULL + 2) * 16)

                blocks(sp, body)

            @block.gpsimd
            def _(pool):
                def body(b):
                    for p in range(PAIRS):
                        pool.wait_ge(e_in[p], (b + 1) * 16)
                        pool.wait_ge(mb_in, (b + 1) * 16)
                        nc.gpsimd.tensor_tensor(ticks[:, p:p + 1], ones32[:], ones32[:], ALU.add).then_inc(e_here, 1)

                blocks(pool, body)

            @block.scalar
            def _(act):
                def exp_e(b, p):
                    W = width(b)
                    act.wait_ge(e_sub, b * NT + p * 2 + 2)
                    e = e_blk[:, bass.ds(p * 2, 2), 0:W]
                    nc.scalar.activation(e, e, ACT.Exp).then_inc(e_ready, 1)

                def t1(b, h, p):
                    W = width(b)
                    g = (b * H + h) * PAIRS + p
                    if isinstance(p, int) and p == 0:
                        act.wait_ge(u_in[h], (b + 1) * 16)
                    act.wait_ge(acc_done, g + 1)
                    for u in range(2):
                        nc.scalar.activation(t_ring[:, g % T_RING, u, 0:W], u_bc[:, h, 0, 0:W], ACT.Copy,
                                             scale=vv4[:, 0, h, bass.ds(p * 2 + u, 1)]).then_inc(t1_ready, 1)

                def step(b, h, p, after=None):
                    W = width(b)
                    g = (b * H + h) * PAIRS + p
                    after = after or ((b, h, p + 1) if not isinstance(p, int) or p < PAIRS - 1 else None)
                    if after:
                        t1(*after)
                    if e_of(b, h, p):
                        exp_e(*e_of(b, h, p))
                    act.wait_ge(hl_free, g + 1)
                    act.wait_ge(p_ready, g + 1)
                    nc.scalar.activation(hl_ring[:, g % HL_RING, 0, :, 0:W], t_ring[:, g % T_RING, :, 0:W],
                                         ACT.Copy).then_inc(hi_ready, 1)

                def evacuate(b, h):
                    W = width(b)
                    q = b * H + h
                    act.wait_ge(o_done, o_before(b, h) + 1)
                    for k in range(KT):
                        if k < KT - 1:
                            act.wait_ge(z_bank, q * (KT - 1) + k + 1)
                        else:
                            act.wait_ge(hl_free, (q + 1) * PAIRS + HL_RING)
                        nc.scalar.activation(z16[:, 0, k, 0:W], z_ps[:, k, 0:W], ACT.Copy,
                                             scale=ZS).then_inc(z_hi, 1)

                def segment(b, h):
                    nxt = seg_next(b, h)
                    for p in range(2, LOOP0):
                        step(b, h, p)
                    with act.Fori(LOOP0, LOOP1) as p:
                        step(b, h, p)
                    for p in range(LOOP1, PAIRS - 1):
                        step(b, h, p)
                    step(b, h, PAIRS - 1, after=nxt and (*nxt, 0))
                    if nxt:
                        for p in range(2):
                            step(*nxt, p)
                    evacuate(b, h)

                exp_e(0, 0)
                t1(0, 0, 0)
                for p in range(2):
                    step(0, 0, p)

                def body(b):
                    for h in range(H):
                        segment(b, h)

                blocks(act, body, first=1)

            @block.vector
            def _(dve):
                nc.vector.memset(credits[:, 6:7], 0.0).then_inc(acc_done, T_RING)
                nc.vector.memset(credits[:, 7:8], 0.0).then_inc(hl_free, HL_RING)
                nc.vector.memset(credits[:, 8:9], 0.0).then_inc(rs_ps, 2)
                nc.vector.memset(credits[:, 9:10], 0.0).then_inc(rs_sb, 1)
                nc.vector.memset(credits[:, 10:11], 0.0).then_inc(o_done, 1)
                nc.vector.memset(credits[:, 11:12], 0.0).then_inc(o_out, 2)

                def lo_part(b, h, p):
                    W = width(b)
                    g = (b * H + h) * PAIRS + p
                    dve.wait_ge(hi_ready, g + 1)
                    nc.vector.tensor_tensor(hl_ring[:, g % HL_RING, 1, :, 0:W], t_ring[:, g % T_RING, :, 0:W],
                                            hl_ring[:, g % HL_RING, 0, :, 0:W], ALU.subtract).then_inc(lo_ready, 1)

                def accumulate(b, h, p):
                    W = width(b)
                    q = b * H + h
                    g = q * PAIRS + p
                    tp = t_ring[:, g % T_RING, :, 0:W]
                    acc = p_acc[:, h % 2, :, 0:W]
                    if isinstance(p, int) and p == 0:
                        dve.wait_ge(rs_ps, q + 1)
                        nc.vector.tensor_scalar(acc, tp, 1.0, None, ALU.mult).then_inc(acc_done, 1)
                    else:
                        dve.wait_ge(acc_done, g + T_RING)
                        nc.vector.tensor_tensor(acc, acc, tp, ALU.add).then_inc(acc_done, 1)

                def subtract_max(b, p):
                    W = width(b)
                    dve.wait_ge(e_here, b * PAIRS + p + 1)
                    for u in range(2):
                        e = e_blk[:, p * 2 + u, 0:W]
                        nc.vector.tensor_tensor(e, e, max_bc[:, 0:W], ALU.subtract).then_inc(e_sub, 1)

                def step(b, h, p, before=None):
                    W = width(b)
                    g = (b * H + h) * PAIRS + p
                    before = before or ((b, h, p - 1) if not isinstance(p, int) or p > 0 else None)
                    tp = t_ring[:, g % T_RING, :, 0:W]
                    for u in range(2):
                        dve.wait_ge(t1_ready, g * 2 + u + 1)
                        tu = t_ring[:, g % T_RING, u, 0:W]
                        nc.vector.scalar_tensor_tensor(out=tu, in0=u_bc[:, h, 1, 0:W],
                                                       scalar=vv4[:, 1, h, bass.ds(p * 2 + u, 1)], in1=tu,
                                                       op0=ALU.mult, op1=ALU.max).then_inc(stt_done, 1)
                    if before:
                        lo_part(*before)
                    if e_of(b, h, p):
                        subtract_max(*e_of(b, h, p))
                    dve.wait_ge(stt_done, g * 2 + 2)
                    if h == 0:
                        dve.wait_ge(e_ready, b * PAIRS + p + 1)
                    nc.vector.tensor_tensor(tp, tp, e_blk[:, bass.ds(p * 2, 2), 0:W], ALU.mult).then_inc(p_ready, 1)
                    if before:
                        accumulate(*before)

                def evacuate_z(b, h):
                    W = width(b)
                    q = b * H + h
                    for k in range(KT):
                        dve.wait_ge(z_hi, q * KT + k + 1)
                        nc.vector.scalar_tensor_tensor(out=z16[:, 1, k, 0:W], in0=z_ps[:, k, 0:W], scalar=ZS,
                                                       in1=z16[:, 0, k, 0:W], op0=ALU.mult,
                                                       op1=ALU.subtract).then_inc(z_lo, 1)

                def row_factors(b, h):
                    q = b * H + h
                    n = width(b) // P
                    dve.wait_ge(rs_ps, q + 3)
                    nc.vector.reciprocal(rinv[:, 0:n], c_ps[:, 0:n]).then_inc(rinv_done, 1)
                    dve.wait_ge(rinv_done, q + 1)
                    nc.vector.tensor_scalar(rcoef[:, 0:n], rinv[:, 0:n], coef0[:], None,
                                            ALU.mult).then_inc(rs_sb, 1)
                    dve.wait_ge(rs_sb, q + 2)
                    if h == 0:
                        dve.wait_ge(x1_in, (b + 1) * 16)

                def add_out(b, h, its):
                    n = width(b) // P
                    for it in its:
                        f = o_before(b, h) + it
                        dve.wait_ge(o_done, f + 2)
                        if h > 0:
                            dve.wait_ge(o_out, f - n + 3)
                        nc.vector.scalar_tensor_tensor(out=out_acc[:, it], in0=o_ps[:, it % 3],
                                                       scalar=rcoef[:, it:it + 1], in1=out_acc[:, it],
                                                       op0=ALU.mult, op1=ALU.add).then_inc(o_out, 1)

                def segment(b, h):
                    for p in range(4, LOOP0):
                        step(b, h, p)
                    with dve.Fori(LOOP0, LOOP1) as p:
                        step(b, h, p)
                    for p in range(LOOP1, PAIRS):
                        step(b, h, p)
                    last = (b, h, PAIRS - 1)
                    nxt = seg_next(b, h)
                    if nxt:
                        step(*nxt, 0, before=last)
                        step(*nxt, 1)
                    else:
                        lo_part(*last)
                        dve.wait_ge(p_ready, (b * H + H) * PAIRS)
                        accumulate(*last)
                    evacuate_z(b, h)
                    if nxt:
                        step(*nxt, 2)
                    row_factors(b, h)
                    add_out(b, h, [0])
                    if nxt:
                        step(*nxt, 3)
                    add_out(b, h, range(1, width(b) // P))

                subtract_max(0, 0)
                for p in range(4):
                    step(0, 0, p)

                def body(b):
                    for h in range(H):
                        segment(b, h)

                blocks(dve, body, first=1)

            @block.tensor
            def _(pe):
                def pair(b, h, p, first=False, last=False, before=None):
                    W = width(b)
                    g = (b * H + h) * PAIRS + p
                    r = g % HL_RING
                    pe.wait_ge(lo_ready, g + 1)
                    for k in range(KT):
                        if before is not None:
                            pe.wait_ge(z_lo, before * KT + k + 1)
                        for u in range(2):
                            hk = [h16[:, s, p * 2 + u, k * P:(k + 1) * P] for s in range(2)]
                            for n, (hs, ps) in enumerate(((0, 0), (0, 1), (1, 0))):
                                mm = nc.tensor.matmul(z_ps[:, k, 0:W], hk[hs], hl_ring[:, r, ps, u, 0:W],
                                                      start=first and u == 0 and n == 0,
                                                      stop=last and u == 1 and n == 2)
                        if k == KT - 1:
                            mm.then_inc(hl_free, 1)
                        elif last:
                            mm.then_inc(z_bank, 1)

                def project(b, h):
                    W = width(b)
                    n = W // P
                    q = b * H + h
                    pe.wait_ge(acc_done, (q + 1) * PAIRS + T_RING)
                    pe.wait_ge(rs_sb, q + 1)
                    for it in range(n):
                        for u in range(2):
                            mm = nc.tensor.matmul(c_ps[:, it:it + 1], p_acc[:, h % 2, u, it * P:(it + 1) * P],
                                                  ones32[:], start=u == 0, stop=u == 1)
                    mm.then_inc(rs_ps, 1)
                    pe.wait_ge(z_lo, (q + 1) * KT)
                    for it in range(n):
                        pe.wait_ge(o_out, o_before(b, h) + 2 + (it >= 3))
                        for k in range(KT):
                            for m, (zs, ws) in enumerate(((0, 0), (0, 1), (1, 0))):
                                mm = nc.tensor.matmul(o_ps[:, it % 3], z16[:, zs, k, it * P:(it + 1) * P],
                                                      w16[:, ws, k, h * D:(h + 1) * D], start=k == 0 and m == 0,
                                                      stop=k == KT - 1 and m == 2)
                        mm.then_inc(o_done, 1)

                def segment(b, h):
                    with pe.Fori(1, PAIRS - 1) as p:
                        pair(b, h, p)
                    pair(b, h, PAIRS - 1, last=True)
                    nxt = seg_next(b, h)
                    if nxt:
                        pair(*nxt, 0, first=True, before=b * H + h)
                    project(b, h)

                pair(0, 0, 0, first=True)

                def body(b):
                    for h in range(H):
                        segment(b, h)

                blocks(pe, body)


def kernel(x, adj, L0_gnn_W, L0_gnn_b, L1_gnn_W, L1_gnn_a):
    import numpy as np
    import concourse.bacc as bacc
    from concourse.bass_utils import run_bass_kernel_spmd

    x, adj = np.asarray(x), np.asarray(adj)
    adjT = adj.T
    adjT = np.concatenate([adjT, adjT[:, N - 1:]], axis=1)
    adjT = np.ascontiguousarray(np.concatenate([adjT, adjT[N - 1:]], axis=0))
    arrays = {
        "x_in": np.ascontiguousarray(np.concatenate([x, x[N - 1:]], axis=0)),
        "adjT_in": adjT,
        "W0_in": np.ascontiguousarray(L0_gnn_W),
        "b0_in": np.ascontiguousarray(L0_gnn_b),
        "W1_in": np.ascontiguousarray(L1_gnn_W),
        "a1_in": np.ascontiguousarray(L1_gnn_a),
    }
    nc = bacc.Bacc("TRN2", target_bir_lowering=False, num_devices=1)
    args = [nc.dram_tensor(name, a.shape, mybir.dt.from_np(a.dtype), kind="ExternalInput").ap()
            for name, a in arrays.items()]
    out = nc.dram_tensor("out_dram", (N, D), F32, kind="ExternalOutput").ap()
    gnn_kernel(nc, *args, out)
    result = run_bass_kernel_spmd(nc, [arrays], core_ids=[0])
    return result.results[0]["out_dram"]
```

```python
from contextlib import ExitStack

import concourse.bass as bass
from concourse import mybir

F32 = mybir.dt.float32
F16 = mybir.dt.float16
ALU = mybir.AluOpType
ACT = mybir.ActivationFunctionType
AX_X = mybir.AxisListType.X
RMAX = bass.bass_isa.ReduceOp.max

N = 3327
P = 128
NT = (N + P - 1) // P
NP = NT * P
LASTP = N - (NT - 1) * P
D = 512
KT = D // P
H = 4
PAIRS = NT // 2
BW = 512
NB = (NP + BW - 1) // BW
FULL = NP // BW
LASTW = NP - FULL * BW
IT = BW // P
EPS = 1e-5
SLOPE = 0.01
HS = 2.0 ** 11
PS = 2.0 ** 15
ZS = 2.0 ** -27
WS = 2.0 ** 15
COEF = 1.0 / (ZS * HS * WS * H)
TINY = 1e-30
LOWEST = -3.0e38

ADJ_RING = 4
A_RING = 2
T_RING = 3
HL_RING = 3


def width(b):
    return BW if not isinstance(b, int) or b < FULL else LASTW


def ring_loop(eng, total, ring, body):
    for slot in range(ring):
        body(slot, slot, 0)
    with eng.Fori(1, total // ring) as turn:
        for slot in range(ring):
            body(turn * ring + slot, slot, turn)
    for slot in range(total % ring):
        body(total // ring * ring + slot, slot, total // ring)


def slot_uses(total, ring, slot):
    return total // ring + (slot < total % ring)


def gnn_kernel(nc, x, adjT, W0, b0, W1, a1, out):
    x1_dram = nc.dram_tensor("x1_dram", (NP, D), F32, kind="Internal").ap()
    rows_dram = nc.dram_tensor("rows_dram", (2 * H + 1, NP), F32, kind="Internal").ap()
    x_t = x.rearrange("(t p) d -> p t d", p=P)
    x1_t = x1_dram.rearrange("(t p) d -> p t d", p=P)
    adj_t = adjT.rearrange("(t p) i -> p t i", p=P)

    with ExitStack() as ctx:
        def sb(name, size, dt):
            return ctx.enter_context(nc.sbuf_tensor(name, [P, size], dt))

        def sem(name):
            return ctx.enter_context(nc.semaphore(name))

        h_reg = sb("h_reg", 2 * NT * D, F16)
        x_reg = sb("x_reg", NT * BW, F32)
        w_reg = sb("w_reg", 2 * KT * H * D, F16)
        ring_reg = sb("ring_reg", 8 * BW, F32)
        z_reg = sb("z_reg", 2 * KT * BW, F16)
        t_reg = sb("t_reg", 2 * T_RING * BW, F32)
        hl_reg = sb("hl_reg", HL_RING * 4 * BW, F16)
        ao_reg = sb("ao_reg", 8 * BW, F32)
        row_reg = sb("row_reg", BW, F32)

        h16 = h_reg[:].rearrange("p (s t d) -> p s t d", s=2, t=NT)
        xs = x_reg[:].rearrange("p (t d) -> p t d", t=NT)
        e_blk = xs
        w16 = w_reg[:].rearrange("p (k h s n) -> p k h s n", k=KT, h=H, s=2)
        w_raw = w_reg[:].bitcast(F32).rearrange("p (k h n) -> p k h n", k=KT, h=H)
        w_scaled = hl_reg[:, NP + 2 * BW:NP + 4 * BW].bitcast(F32)
        a_bc = xs[:, 4 * IT:4 * IT + 2 * H]
        adj_ring = ring_reg[:].rearrange("p (s u i) -> p s u i", s=ADJ_RING, u=2)
        a_ring = t_reg[:, 0:2 * BW].bitcast(F16).rearrange("p (s u i) -> p s u i", s=A_RING, u=2)
        w0_sb = t_reg[:, 2 * BW:6 * BW].rearrange("p (k n) -> p k n", k=KT)
        s0t = z_reg[:].bitcast(F32).rearrange("p (k i) -> p k i", k=KT)
        adj_max = ao_reg[:, 0:NP]
        adj_cnt = hl_reg[:, 0:NP]
        b0_bc = row_reg[:]
        x_ring = t_reg[:].rearrange("p (s u d) -> p s u d", s=3, u=2)
        ln1_stage = ring_reg[:].rearrange("p (s u d) -> p s u d", s=4, u=2)
        ht_ring = hl_reg[:].bitcast(F32).rearrange("p (s k i) -> p s k i", s=6, k=KT)
        u_bc = ring_reg[:].rearrange("p (h q i) -> p h q i", h=H, q=2)
        z16 = z_reg[:].rearrange("p (s k i) -> p s k i", s=2, k=KT)
        t_ring = x_ring
        hl_ring = hl_reg[:].rearrange("p (r s u i) -> p r s u i", r=HL_RING, s=2, u=2)
        p_acc = ao_reg[:, 0:4 * BW].rearrange("p (a u i) -> p a u i", a=2, u=2)
        out_acc = ao_reg[:, 4 * BW:8 * BW].rearrange("p (t d) -> p t d", t=IT)
        max_bc = row_reg[:]

        ident = sb("ident", P, F32)
        ones32 = sb("ones32", 1, F32)
        ones16 = sb("ones16", 1, F16)
        valid = sb("valid", NT, F32)
        invalid = sb("invalid", 1, F32)
        junk = hl_reg[:, NP:NP + 2 * BW].rearrange("p (u i) -> p u i", u=2)
        credits = sb("credits", 16, F32)
        ticks = sb("ticks", PAIRS, F32)
        bst = sb("bst", NT * 6, F32)
        mv = sb("mv", NT * 2, F32)
        ve = sb("ve", NT, F32)
        sd = sb("sd", NT, F32)
        y0 = sb("y0", NT, F32)
        y1 = sb("y1", NT, F32)
        rs = sb("rs", NT, F32)
        nb = sb("nb", NT, F32)
        wa = sb("wa", KT * 2 * H, F32)
        wmx = ao_reg[:, 4 * BW * 2 - KT * H:]
        wmx1 = sb("wmx1", 1, F32)
        wmax = sb("wmax", 1, F32)
        wsc = sb("wsc", 1, F32)
        coef0 = sb("coef0", 1, F32)
        degp = sb("degp", NT * NB, F32)
        deg = sb("deg", NT, F32)
        rdeg = sb("rdeg", NT, F32)
        cnt_col = sb("cnt_col", IT, F32)
        sdc = ao_reg[:, NP:NP + NT * 2 * H]
        dmx = sb("dmx", 2 * H, F32)
        dall = sb("dall", 2 * H, F32)
        dn = ao_reg[:, NP + NT * 2 * H:NP + NT * 3 * H]
        vv = sb("vv", 2 * H * NT, F32)
        qq = sb("qq", NT, F32)
        lk = sb("lk", NT, F32)
        rows = sb("rows", (2 * H + 1) * NT, F32)
        rinv = sb("rinv", 2 * IT, F32)
        rcoef = sb("rcoef", IT, F32)

        mv3 = mv[:].rearrange("p (t c) -> p t c", c=2)
        bst3 = bst[:].rearrange("p (t c) -> p t c", c=6)
        wa3 = wa[:].rearrange("p (k r) -> p k r", k=KT)
        degp3 = degp[:].rearrange("p (t b) -> p t b", b=NB)
        sdc3 = sdc.rearrange("p (t r) -> p t r", r=2 * H)
        dn3 = dn.rearrange("p (h t) -> p h t", h=H)
        vv4 = vv[:].rearrange("p (q h t) -> p q h t", q=2, h=H)
        rows3 = rows[:].rearrange("p (r t) -> p r t", t=NT)

        z_ps = ctx.enter_context(nc.psum_tensor("z_ps", [P, KT, 512], F32))
        o_ps = ctx.enter_context(nc.psum_tensor("o_ps", [P, 3, 512], F32))
        c_ps = ctx.enter_context(nc.psum_tensor("c_ps", [P, 512], F32))

        s_var = sem("s_var")
        s_sqrt = sem("s_sqrt")
        s_ln = sem("s_ln")
        dve_step = sem("dve_step")
        steps = [0]

        def link(dve, ins):
            steps[0] += 1
            ins.then_inc(dve_step, 1)
            dve.wait_ge(dve_step, steps[0])

        def ln_stats(dve, t0, t1, written, count):
            dve.wait_ge(written, t1)
            for t in range(t0, t1):
                nc.vector.bn_aggr(mv3[:, t], bst3[:, t]).then_inc(count, 1)
            dve.wait_ge(count, t1)
            nc.vector.tensor_scalar(ve[:, t0:t1], mv3[:, t0:t1, 1], EPS, None, ALU.add).then_inc(s_var, 1)

        def ln_scalars(dve, t0, t1, group):
            c = slice(t0, t1)
            dve.wait_ge(s_sqrt, group + 1)
            link(dve, nc.vector.reciprocal(y0[:, c], sd[:, c]))
            link(dve, nc.vector.tensor_tensor(y1[:, c], y0[:, c], y0[:, c], ALU.mult))
            link(dve, nc.vector.tensor_tensor(y1[:, c], y1[:, c], ve[:, c], ALU.mult))
            link(dve, nc.vector.tensor_scalar(y1[:, c], y1[:, c], -0.5, 1.5, ALU.mult, ALU.add))
            link(dve, nc.vector.scalar_tensor_tensor(out=rs[:, c], in0=y1[:, c], scalar=HS, in1=y0[:, c],
                                                     op0=ALU.mult, op1=ALU.mult))
            nc.vector.scalar_tensor_tensor(out=nb[:, c], in0=mv3[:, c, 0], scalar=-1.0, in1=rs[:, c],
                                           op0=ALU.mult, op1=ALU.mult).then_inc(s_ln, 1)

        def ln_sqrt(act, t0, t1, group):
            act.wait_ge(s_var, group + 1)
            nc.scalar.activation(sd[:, t0:t1], ve[:, t0:t1], ACT.Sqrt).then_inc(s_sqrt, 1)

        groups0 = [(0, 4), (4, 10), (10, 18), (18, NT)]
        x_in = [sem(f"x_in{c}") for c in range(len(groups0))]
        w_in = [sem(f"w_in{k}") for k in range(KT)]
        a_in = sem("a_in")
        s_bst = sem("s_bst")
        s_mv = sem("s_mv")
        s_const = sem("s_const")
        s_ident0 = sem("s_ident0")
        h0_relu = sem("h0_relu")
        h0_hi = sem("h0_hi")
        h0_lo = sem("h0_lo")
        s_wred = sem("s_wred")
        s_wmx = sem("s_wmx")
        s_wmax = sem("s_wmax")
        s_wsc = sem("s_wsc")
        w_step = sem("w_step")
        adj_in = [sem(f"adj_in{s}") for s in range(ADJ_RING)]
        w0_in = sem("w0_in")
        b0_in = sem("b0_in")
        mx_done = sem("mx_done")
        cnt_done = sem("cnt_done")
        a_ready = sem("a_ready")
        a_pe = sem("a_pe")
        a_act = sem("a_act")
        s0_bank = sem("s0_bank")
        s0_out = sem("s0_out")
        cnt_ps = sem("cnt_ps")
        cnt_sb = sem("cnt_sb")
        o0_done = sem("o0_done")
        o0_out = sem("o0_out")
        MX0 = 2 * (ADJ_RING + 1)

        with nc.Block() as block:
            @block.sync
            def _(sp):
                def load(b, p, slot, turn):
                    W = width(b)
                    g = b * PAIRS + p
                    sp.wait_ge(mx_done, MX0 + 2 * (g - back(slot, turn)) + 2)
                    sp.dma_start(adj_ring[:, slot, :, 0:W],
                                 adj_t[:, bass.ds(p * 2, 2), bass.ds(b * BW, W)]).then_inc(adj_in[slot], 16)

                def back(slot, turn):
                    if isinstance(turn, int) and turn == 0:
                        return 1 if slot == 0 else ADJ_RING + 1
                    return ADJ_RING

                def block_loads(b, first=0):
                    for slot in range(first, ADJ_RING):
                        load(b, slot, slot, 0)
                    with sp.Fori(1, PAIRS // ADJ_RING) as turn:
                        for slot in range(ADJ_RING):
                            load(b, turn * ADJ_RING + slot, slot, turn)
                    load(b, PAIRS - 1, 0, PAIRS // ADJ_RING)

                for c, (t0, t1) in enumerate(groups0):
                    sp.dma_start(xs[:, t0:t1, :], x_t[:, t0:t1, :]).then_inc(x_in[c], 16)
                for slot in range(ADJ_RING):
                    load(0, slot, slot, 0)
                sp.dma_start(w0_sb, W0.rearrange("(k p) n -> p k n", p=P)).then_inc(w0_in, 16)
                sp.dma_start(b0_bc, b0.partition_broadcast(P)).then_inc(b0_in, 16)
                for k in range(KT):
                    sp.dma_start(w_raw[:, k], W1[k * P:(k + 1) * P, :].rearrange("p (h n) -> p h n", h=H)
                                 ).then_inc(w_in[k], 16)
                block_loads(0, first=ADJ_RING)
                sp.wait_ge(h0_lo, PAIRS)
                sp.dma_start(a_bc, a1.rearrange("h (q c) o -> (h q) (c o)", q=2)
                             .partition_broadcast(P)).then_inc(a_in, 16)
                with sp.Fori(1, FULL) as b:
                    block_loads(b)
                block_loads(FULL)

            @block.gpsimd
            def _(pool):
                nc.gpsimd.memset(ident[:], 0.0).then_inc(s_ident0, 1)
                nc.gpsimd.memset(valid[:], 1.0).then_inc(s_ident0, 1)
                pool.wait_ge(s_ident0, 2)
                nc.gpsimd.affine_select(out=ident[:], in_=ident[:], compare_op=ALU.not_equal, fill=1.0,
                                        base=0, pattern=[[-1, P]], channel_multiplier=1).then_inc(s_const, 1)
                nc.gpsimd.affine_select(out=valid[:, NT - 1:NT], in_=valid[:, NT - 1:NT],
                                        compare_op=ALU.is_ge, fill=0.0, base=LASTP - 1, pattern=[[0, 1]],
                                        channel_multiplier=-1).then_inc(s_const, 1)
                pool.wait_ge(s_wmx, 1)
                nc.gpsimd.partition_all_reduce(wmax[:], wmx1[:], P, RMAX).then_inc(s_wmax, 1)
                pool.wait_ge(s_wsc, 1)
                for n in range(KT * H):
                    k, h = n // H, n % H
                    if n > 0:
                        pool.wait_ge(w_step, 3 * n)
                    nc.gpsimd.tensor_scalar(w_scaled, w_raw[:, k, h], wsc[:], None, ALU.mult).then_inc(w_step, 1)
                    pool.wait_ge(w_step, 3 * n + 1)
                    nc.gpsimd.tensor_copy(w16[:, k, h, 0], w_scaled).then_inc(w_step, 1)
                    pool.wait_ge(w_step, 3 * n + 2)
                    nc.gpsimd.tensor_tensor(w16[:, k, h, 1], w_scaled, w16[:, k, h, 0],
                                            ALU.subtract).then_inc(w_step, 1)

            @block.vector
            def _(dve):
                nc.vector.memset(ones32[:], 1.0)
                nc.vector.memset(ones16[:], 1.0).then_inc(a_pe, A_RING)
                nc.vector.memset(credits[:, 1:2], 0.0).then_inc(a_act, 2 * A_RING)
                nc.vector.memset(credits[:, 3:4], 0.0).then_inc(cnt_sb, 1)
                nc.vector.memset(credits[:, 4:5], 0.0).then_inc(o0_out, 2)
                nc.vector.memset(credits[:, 5:6], 0.0).then_inc(o0_done, 1)
                nc.vector.memset(adj_cnt.bitcast(F32), 0.0).then_inc(cnt_done, 1)
                nc.vector.memset(adj_max, LOWEST).then_inc(mx_done, MX0)

                def pair(b, p, slot, turn):
                    W = width(b)
                    g = b * PAIRS + p
                    cols = bass.ds(b * BW, W)
                    dve.wait_ge(adj_in[slot], (b * slot_uses(PAIRS, ADJ_RING, slot) + turn + 1) * 16)
                    dve.wait_ge(a_pe, g + 1)
                    dve.wait_ge(a_act, g * 2 + 2)
                    for u in range(2):
                        nc.vector.tensor_scalar(a_ring[:, g % A_RING, u, 0:W], adj_ring[:, slot, u, 0:W], 0.0,
                                                valid[:, bass.ds(p * 2 + u, 1)], ALU.not_equal,
                                                ALU.mult).then_inc(a_ready, 1)
                    for u in range(2):
                        dve.wait_ge(mx_done, g * 2 + MX0 + u)
                        nc.vector.tensor_tensor(adj_max[:, cols], adj_max[:, cols], adj_ring[:, slot, u, 0:W],
                                                ALU.max).then_inc(mx_done, 1)
                        dve.wait_ge(a_ready, g * 2 + u + 1)
                        dve.wait_ge(cnt_done, g * 2 + u + 1)
                        nc.vector.tensor_tensor(adj_cnt[:, cols], adj_cnt[:, cols], a_ring[:, g % A_RING, u, 0:W],
                                                ALU.add).then_inc(cnt_done, 1)

                def head(b):
                    for p in range(3):
                        pair(b, p, p, 0)

                def rest(b):
                    pair(b, 3, 3, 0)
                    with dve.Fori(1, PAIRS // ADJ_RING) as turn:
                        for slot in range(ADJ_RING):
                            pair(b, turn * ADJ_RING + slot, slot, turn)
                    pair(b, PAIRS - 1, 0, PAIRS // ADJ_RING)

                def evacuate(b):
                    W = width(b)
                    n = W // P
                    dve.wait_ge(cnt_ps, b + 1)
                    nc.vector.tensor_copy(cnt_col[:, 0:n], c_ps[:, 0:n]).then_inc(cnt_sb, 1)
                    dve.wait_ge(cnt_sb, b + 2)
                    for it in range(n):
                        f = b * IT + it
                        dve.wait_ge(o0_done, f + 2)
                        nc.vector.scalar_tensor_tensor(out=xs[:, f], in0=b0_bc, scalar=cnt_col[:, it:it + 1],
                                                       in1=o_ps[:, it % 2], op0=ALU.mult,
                                                       op1=ALU.add).then_inc(o0_out, 1)

                def stats(c):
                    t0, t1 = groups0[c]
                    dve.wait_ge(x_in[c], 16)
                    for t in range(t0, t1):
                        nc.vector.bn_stats(bst3[:, t], xs[:, t]).then_inc(s_bst, 1)
                    ln_stats(dve, t0, t1, s_bst, s_mv)
                    ln_scalars(dve, t0, t1, c)

                def first_block(c):
                    t0, t1 = groups0[c]
                    for p in range(t0 // 2, t1 // 2):
                        dve.wait_ge(h0_hi, p + 1)
                        nc.vector.tensor_tensor(h16[:, 1, 2 * p:2 * p + 2], xs[:, 2 * p:2 * p + 2],
                                                h16[:, 0, 2 * p:2 * p + 2], ALU.subtract).then_inc(h0_lo, 1)
                        if p == 0:
                            dve.wait_ge(s_const, 2)
                        pair(0, p, p % ADJ_RING, p // ADJ_RING)

                def w1_chunk(n):
                    k, h = n // H, n % H
                    if h == 0:
                        dve.wait_ge(w_in[k], 16)
                    nc.vector.tensor_reduce(wmx[:, n:n + 1], w_raw[:, k, h], AX_X, ALU.max,
                                            apply_absolute_value=True).then_inc(s_wred, 1)
                    for r in (2 * h, 2 * h + 1):
                        link(dve, nc.vector.tensor_tensor_reduce(
                            out=w_scaled, in0=w_raw[:, k, h], in1=a_bc[:, r], scale=1.0, scalar=0.0,
                            op0=ALU.mult, op1=ALU.add, accum_out=wa3[:, k, r:r + 1]))

                def w1_scale():
                    dve.wait_ge(s_wmax, 1)
                    link(dve, nc.vector.tensor_scalar(wmax[:], wmax[:], TINY, None, ALU.max))
                    link(dve, nc.vector.reciprocal(wsc[:], wmax[:]))
                    nc.vector.tensor_scalar(coef0[:], wmax[:], COEF, None, ALU.mult)
                    link(dve, nc.vector.tensor_scalar(invalid[:], valid[:, NT - 1:NT], -1.0, 1.0, ALU.mult,
                                                      ALU.add))
                    nc.vector.tensor_scalar(wsc[:], wsc[:], WS, None, ALU.mult).then_inc(s_wsc, 1)

                stats(0)
                stats(1)
                for c in range(len(groups0)):
                    first_block(c)
                    if c + 2 < len(groups0):
                        stats(c + 2)
                dve.wait_ge(b0_in, 16)
                for p in range(3):
                    pair(1, p, p, 0)
                evacuate(0)
                dve.wait_ge(a_in, 16)
                for p in range(3, PAIRS):
                    w1_chunk(p - 3)
                    pair(1, p, p % ADJ_RING, p // ADJ_RING)
                head(2)
                evacuate(1)
                for p in range(PAIRS - 3, KT * H):
                    w1_chunk(p)
                dve.wait_ge(s_wred, KT * H)
                nc.vector.tensor_reduce(wmx1[:], wmx, AX_X, ALU.max).then_inc(s_wmx, 1)
                for b in (2,):
                    rest(b)
                    head(b + 1)
                    w1_scale()
                    evacuate(b)
                with dve.Fori(3, FULL - 1) as b:
                    rest(b)
                    head(b + 1)
                    evacuate(b)
                for b in (FULL - 1, FULL):
                    rest(b)
                    if b < FULL:
                        head(b + 1)
                    evacuate(b)

            @block.scalar
            def _(act):
                def relu(c):
                    t0, t1 = groups0[c]
                    act.wait_ge(s_ln, c + 1)
                    for t in range(t0, t1):
                        nc.scalar.activation(xs[:, t], xs[:, t], ACT.Relu, bias=nb[:, t:t + 1],
                                             scale=rs[:, t:t + 1]).then_inc(h0_relu, 1)
                        if t % 2:
                            act.wait_ge(h0_relu, t + 1)
                            nc.scalar.activation(h16[:, 0, t - 1:t + 1], xs[:, t - 1:t + 1],
                                                 ACT.Copy).then_inc(h0_hi, 1)

                def degrees(b, p):
                    W = width(b)
                    Wv = W if W == BW else W - (NP - N)
                    g = b * PAIRS + p
                    for u in range(2):
                        act.wait_ge(a_ready, g * 2 + u + 1)
                        act.wait_ge(a_act, g * 2 + u + 2 * A_RING - 1)
                        nc.scalar.activation(junk[:, u, 0:Wv], a_ring[:, g % A_RING, u, 0:Wv], ACT.Copy,
                                             accum_out=degp3[:, bass.ds(p * 2 + u, 1), b]).then_inc(a_act, 1)

                def evacuate(b):
                    W = width(b)
                    act.wait_ge(o0_done, b * IT + 1)
                    for k in range(KT):
                        if k < KT - 1:
                            act.wait_ge(s0_bank, b * (KT - 1) + k + 1)
                        else:
                            act.wait_ge(a_pe, (b + 1) * PAIRS + A_RING)
                        nc.scalar.activation(s0t[:, k, 0:W], z_ps[:, k, 0:W], ACT.Copy,
                                             scale=1.0 / HS).then_inc(s0_out, 1)

                for c in range(2):
                    ln_sqrt(act, *groups0[c], c)
                    relu(c)
                for c, (t0, t1) in enumerate(groups0):
                    for p in range(t0 // 2, t1 // 2):
                        degrees(0, p)
                    if c + 2 < len(groups0):
                        ln_sqrt(act, *groups0[c + 2], c + 2)
                        relu(c + 2)
                evacuate(0)
                with act.Fori(1, FULL) as b:
                    with act.Fori(0, PAIRS) as p:
                        degrees(b, p)
                    evacuate(b)
                with act.Fori(0, PAIRS) as p:
                    degrees(FULL, p)
                evacuate(FULL)

            @block.tensor
            def _(pe):
                def pair(b, p, first=False, last=False, evacuated=None):
                    W = width(b)
                    g = b * PAIRS + p
                    if isinstance(b, int) and b == 0:
                        pe.wait_ge(h0_lo, p + 1)
                    pe.wait_ge(a_ready, g * 2 + 2)
                    for k in range(KT):
                        if evacuated is not None:
                            pe.wait_ge(s0_out, evacuated * KT + k + 1)
                        for u in range(2):
                            for s in range(2):
                                mm = nc.tensor.matmul(
                                    z_ps[:, k, 0:W], h16[:, s, p * 2 + u, k * P:(k + 1) * P],
                                    a_ring[:, g % A_RING, u, 0:W], start=first and u == 0 and s == 0,
                                    stop=last and u == 1 and s == 1)
                        if k == KT - 1:
                            mm.then_inc(a_pe, 1)
                        elif last:
                            mm.then_inc(s0_bank, 1)

                def project(b):
                    W = width(b)
                    n = W // P
                    pe.wait_ge(cnt_done, (b + 1) * NT + 1)
                    pe.wait_ge(cnt_sb, b + 1)
                    for it in range(n):
                        mm = nc.tensor.matmul(c_ps[:, it:it + 1], adj_cnt[:, bass.ds(b * BW + it * P, P)], ones16[:],
                                              start=True, stop=True)
                    mm.then_inc(cnt_ps, 1)
                    pe.wait_ge(s0_out, (b + 1) * KT)
                    for it in range(n):
                        f = b * IT + it
                        pe.wait_ge(o0_out, f + 1)
                        for k in range(KT):
                            mm = nc.tensor.matmul(o_ps[:, it % 2], s0t[:, k, it * P:(it + 1) * P], w0_sb[:, k],
                                                  start=k == 0, stop=k == KT - 1)
                        mm.then_inc(o0_done, 1)

                pe.wait_ge(w0_in, 16)
                pair(0, 0, first=True)

                def body(b):
                    with pe.Fori(1, PAIRS - 1) as p:
                        pair(b, p)
                    pair(b, PAIRS - 1, last=True)
                    pair(b + 1, 0, first=True, evacuated=b)
                    project(b)

                body(0)
                with pe.Fori(1, FULL - 1) as b:
                    body(b)
                for b in (FULL - 1, FULL):
                    with pe.Fori(1, PAIRS - 1) as p:
                        pair(b, p)
                    pair(b, PAIRS - 1, last=True)
                    if b < FULL:
                        pair(b + 1, 0, first=True, evacuated=b)
                    project(b)

        x_in1 = [sem(f"x_in1_{s}") for s in range(3)]
        x1_ready = sem("x1_ready")
        x1_bst = sem("x1_bst")
        s_mv1 = sem("s_mv1")
        x1_out = sem("x1_out")
        mt_ps = sem("mt_ps")
        mt_red = sem("mt_red")
        st1_ready = sem("st1_ready")
        st1_split = sem("st1_split")
        hi1_done = sem("hi1_done")
        tr_ps = sem("tr_ps")
        tr_sb = sem("tr_sb")
        sd_ps = sem("sd_ps")
        s_dmx = sem("s_dmx")
        s_dall = sem("s_dall")
        s_dn = sem("s_dn")
        s_vv = sem("s_vv")
        s_uarg = sem("s_uarg")
        s_uexp = sem("s_uexp")
        s_rows = sem("s_rows")
        rt_ps = sem("rt_ps")
        rt_sb = sem("rt_sb")
        rows_out = sem("rows_out")
        groups1 = [(0, 6), (6, 12), (12, 20), (20, NT)]
        NR = 2 * H + 1
        RH = NR * NT // 2
        max_groups = [(t, min(t + IT, NT)) for t in range(0, NT, IT)]
        row_stage = row_reg[:, 0:2 * P].rearrange("p (a i) -> p a i", a=2)

        with nc.Block() as block:
            @block.sync
            def _(sp):
                def load(p, slot, turn):
                    if not (isinstance(turn, int) and turn == 0):
                        sp.wait_ge(x1_ready, p * 2 - 4)
                    sp.dma_start(x_ring[:, slot], x_t[:, bass.ds(p * 2, 2), :]).then_inc(x_in1[slot], 16)

                def store(p):
                    sp.wait_ge(x1_ready, p * 2 + 2)
                    sp.dma_start(x1_t[:, bass.ds(p * 2, 2), :], xs[:, bass.ds(p * 2, 2)]).then_inc(x1_out, 16)

                for p in range(3):
                    load(p, p, 0)
                with sp.Fori(1, PAIRS // 3) as turn:
                    for slot in range(3):
                        load(turn * 3 + slot, slot, turn)
                        store(turn * 3 + slot - 3)
                load(PAIRS - 1, 0, PAIRS // 3)
                for p in range(PAIRS - 4, PAIRS):
                    store(p)
                sp.wait_ge(rt_sb, 2)
                rows_v = rows_dram.rearrange("r (t i) -> (r t) i", i=P)
                for a in range(2):
                    sp.dma_start(rows_v[a * RH:(a + 1) * RH, :], row_stage[0:RH, a]).then_inc(rows_out, 16)
                sp.wait_ge(rows_out, 32)
                sp.wait_ge(x1_out, 16 * PAIRS)

            @block.gpsimd
            def _(pool):
                pool.wait_ge(s_dmx, 1)
                nc.gpsimd.partition_all_reduce(dall[:], dmx[:], P, RMAX).then_inc(s_dall, 1)

            @block.scalar
            def _(act):
                def transposed(t):
                    act.wait_ge(tr_ps, t + 1)
                    if t >= 6:
                        act.wait_ge(sd_ps, t - 5)
                    nc.scalar.activation(ht_ring[:, t % 6], o_ps[:, t % 3]
                                         .rearrange("p (k i) -> p k i", k=KT), ACT.Copy).then_inc(tr_sb, 1)

                for c, (t0, t1) in enumerate(groups1):
                    ln_sqrt(act, t0, t1, len(groups0) + c)
                    act.wait_ge(s_ln, len(groups0) + c + 1)
                    for t in range(t0, t1):
                        p = t // 2
                        if t % 2 == 0 and p >= 4:
                            act.wait_ge(st1_split, p - 3)
                            act.wait_ge(tr_ps, 2 * (p - 3))
                        nc.scalar.activation(ln1_stage[:, p % 4, t % 2], xs[:, t], ACT.Relu, bias=nb[:, t:t + 1],
                                             scale=rs[:, t:t + 1]).then_inc(st1_ready, 1)
                        if t % 2:
                            act.wait_ge(st1_ready, t + 1)
                            nc.scalar.activation(h16[:, 0, t - 1:t + 1], ln1_stage[:, p % 4],
                                                 ACT.Copy).then_inc(hi1_done, 1)
                        if t > 0:
                            transposed(t - 1)
                transposed(NT - 1)
                for h in range(H):
                    act.wait_ge(s_dn, h + 1)
                    for q, f in ((0, 1.0), (1, SLOPE)):
                        nc.scalar.activation(vv4[:, q, h], dn3[:, h], ACT.Exp, scale=f).then_inc(s_vv, 1)
                act.wait_ge(s_uarg, 2 * H)
                nc.scalar.activation(rows[:, 0:2 * H * NT], rows[:, 0:2 * H * NT], ACT.Exp).then_inc(s_uexp, 1)
                for a in range(2):
                    act.wait_ge(rt_ps, a + 1)
                    nc.scalar.activation(row_stage[0:RH, a], o_ps[0:RH, a, 0:P], ACT.Copy).then_inc(rt_sb, 1)

            @block.tensor
            def _(pe):
                def transpose_max(n):
                    t0, t1 = max_groups[n]
                    if n >= KT:
                        pe.wait_ge(mt_red, n - KT + 1)
                    for t in range(t0, t1):
                        mm = nc.tensor.transpose(z_ps[:, n % KT, (t - t0) * P:(t - t0 + 1) * P],
                                                 adj_max[:, t * P:(t + 1) * P], ident[:])
                    mm.then_inc(mt_ps, 1)

                for n in range(KT):
                    transpose_max(n)

                def scores(t):
                    pe.wait_ge(tr_sb, t + 1)
                    for k in range(KT):
                        mm = nc.tensor.matmul(c_ps[:, t * 2 * H:(t + 1) * 2 * H], ht_ring[:, t % 6, k], wa3[:, k],
                                              start=k == 0, stop=k == KT - 1)
                    mm.then_inc(sd_ps, 1)

                for t in range(NT):
                    pe.wait_ge(st1_ready, t + 1)
                    if t >= 3:
                        pe.wait_ge(tr_sb, t - 2)
                    for k in range(KT):
                        mm = nc.tensor.transpose(o_ps[:, t % 3, k * P:(k + 1) * P],
                                                 ln1_stage[:, (t // 2) % 4, t % 2, k * P:(k + 1) * P], ident[:])
                    mm.then_inc(tr_ps, 1)
                    if t >= 1:
                        scores(t - 1)
                scores(NT - 1)
                for n in range(KT, len(max_groups)):
                    transpose_max(n)
                pe.wait_ge(s_rows, 1)
                pe.wait_ge(tr_sb, NT)
                for a in range(2):
                    nc.tensor.transpose(o_ps[0:RH, a, 0:P], rows[:, a * RH:(a + 1) * RH],
                                        ident[:]).then_inc(rt_ps, 1)

            @block.vector
            def _(dve):
                link(dve, nc.vector.tensor_reduce(deg[:], degp3, AX_X, ALU.add))
                link(dve, nc.vector.tensor_tensor(deg[:, NT - 1:NT], deg[:, NT - 1:NT], invalid[:], ALU.add))
                link(dve, nc.vector.reciprocal(rdeg[:], deg[:]))

                def x1_pair(p, slot, turn):
                    dve.wait_ge(x_in1[slot], (turn + 1) * 16)
                    for u in range(2):
                        t = p * 2 + u
                        nc.vector.scalar_tensor_tensor(out=xs[:, t], in0=xs[:, t], scalar=rdeg[:, bass.ds(t, 1)],
                                                       in1=x_ring[:, slot, u], op0=ALU.mult,
                                                       op1=ALU.add).then_inc(x1_ready, 1)
                    for u in range(2):
                        t = p * 2 + u
                        dve.wait_ge(x1_ready, t + 1)
                        nc.vector.bn_stats(bst3[:, t], xs[:, t]).then_inc(x1_bst, 1)

                def reduce_max(n):
                    t0, t1 = max_groups[n]
                    dve.wait_ge(mt_ps, n + 1)
                    nc.vector.tensor_reduce(rows3[:, 2 * H, t0:t1],
                                            z_ps[:, n % KT, 0:(t1 - t0) * P].rearrange("p (t i) -> p t i", i=P),
                                            AX_X, ALU.max).then_inc(mt_red, 1)

                def split(c):
                    t0, t1 = groups1[c]
                    for p in range(t0 // 2, t1 // 2):
                        dve.wait_ge(hi1_done, p + 1)
                        nc.vector.tensor_tensor(h16[:, 1, 2 * p:2 * p + 2], ln1_stage[:, p % 4],
                                                h16[:, 0, 2 * p:2 * p + 2], ALU.subtract).then_inc(st1_split, 1)

                for c, (t0, t1) in enumerate(groups1):
                    for p in range(t0 // 2, t1 // 2):
                        x1_pair(p, p % 3, p // 3)
                    ln_stats(dve, t0, t1, x1_bst, s_mv1)
                    if c > 0:
                        split(c - 1)
                    ln_scalars(dve, t0, t1, len(groups0) + c)
                for n in range(KT):
                    reduce_max(n)
                split(len(groups1) - 1)
                dve.wait_ge(sd_ps, NT)
                link(dve, nc.vector.tensor_scalar(sdc, c_ps[:, 0:NT * 2 * H], 1.0 / HS, None, ALU.mult))
                nc.vector.tensor_reduce(dmx[:], sdc.rearrange("p (t r) -> p r t", r=2 * H), AX_X,
                                        ALU.max).then_inc(s_dmx, 1)
                dve.wait_ge(s_dall, 1)
                for h in range(H):
                    nc.vector.tensor_scalar(dn3[:, h], sdc3[:, :, 2 * h + 1], dall[:, 2 * h + 1:2 * h + 2], None,
                                            ALU.subtract).then_inc(s_dn, 1)
                for h in range(H):
                    link(dve, nc.vector.tensor_scalar(qq[:], sdc3[:, :, 2 * h], dall[:, 2 * h + 1:2 * h + 2], None,
                                                      ALU.add))
                    link(dve, nc.vector.scalar_tensor_tensor(out=lk[:], in0=qq[:], scalar=SLOPE, in1=qq[:],
                                                             op0=ALU.mult, op1=ALU.max))
                    nc.vector.tensor_tensor(rows3[:, 2 * h], qq[:], lk[:], ALU.subtract).then_inc(s_uarg, 1)
                    nc.vector.scalar_tensor_tensor(out=rows3[:, 2 * h + 1], in0=qq[:], scalar=SLOPE, in1=lk[:],
                                                   op0=ALU.mult, op1=ALU.subtract).then_inc(s_uarg, 1)
                    dve.wait_ge(s_uarg, 2 * h + 2)
                for n in range(KT, len(max_groups)):
                    reduce_max(n)
                dve.wait_ge(s_vv, 2 * H)
                link(dve, nc.vector.tensor_scalar(vv[:].rearrange("p (r t) -> p r t", t=NT)[:, :, NT - 1],
                                                  vv[:].rearrange("p (r t) -> p r t", t=NT)[:, :, NT - 1],
                                                  valid[:, NT - 1:NT], None, ALU.mult))
                dve.wait_ge(s_uexp, 1)
                nc.vector.tensor_scalar(rows[:, 0:2 * H * NT], rows[:, 0:2 * H * NT], PS, None,
                                        ALU.mult).then_inc(s_rows, 1)

        u_in = [sem(f"u_in{h}") for h in range(H)]
        e_in = [sem(f"e_in{p}") for p in range(PAIRS)]
        mb_in = sem("mb_in")
        x1_in = sem("x1_in")
        out_st = sem("out_st")
        e_here = sem("e_here")
        e_sub = sem("e_sub")
        e_ready = sem("e_ready")
        t1_ready = sem("t1_ready")
        stt_done = sem("stt_done")
        p_ready = sem("p_ready")
        acc_done = sem("acc_done")
        hi_ready = sem("hi_ready")
        lo_ready = sem("lo_ready")
        hl_free = sem("hl_free")
        z_bank = sem("z_bank")
        z_hi = sem("z_hi")
        z_lo = sem("z_lo")
        rs_ps = sem("rs_ps")
        rs_sb = sem("rs_sb")
        rinv_done = sem("rinv_done")
        o_done = sem("o_done")
        o_out = sem("o_out")
        LOOP0, LOOP1 = 5, PAIRS - 2
        E_LATE = PAIRS - LOOP1
        assert LOOP1 - LOOP0 + (LOOP1 - LOOP0 + 1) == PAIRS

        def seg_next(b, h):
            return (b, h + 1) if h < H - 1 else ((b + 1, 0) if not isinstance(b, int) or b < FULL else None)

        def o_before(b, h):
            if isinstance(b, int) and b == FULL:
                return FULL * H * IT + h * (LASTW // P)
            return (b * H + h) * IT

        def e_of(b, h, p):
            looped = not isinstance(p, int)
            if h == 0 and isinstance(b, int) and b == 0:
                return (b, p + 1) if looped or p < PAIRS - 1 else None
            if h == 0:
                return (b, p + E_LATE) if looped or p == LOOP0 - 1 else None
            if h == H - 1 and (not isinstance(b, int) or b < FULL):
                return (b + 1, p - LOOP0) if looped else None
            return None

        def blocks(eng, body, first=0):
            for b in range(first):
                body(b)
            with eng.Fori(first, FULL - 1) as b:
                body(b)
            body(FULL - 1)
            body(FULL)

        with nc.Block() as block:
            @block.sync
            def _(sp):
                def load_u(b, h):
                    W = width(b)
                    sp.dma_start(u_bc[:, h, :, 0:W], rows_dram[2 * h:2 * h + 2, bass.ds(b * BW, W)]
                                 .partition_broadcast(P)).then_inc(u_in[h], 16)

                def load_max(b):
                    W = width(b)
                    sp.dma_start(max_bc[:, 0:W], rows_dram[2 * H, bass.ds(b * BW, W)]
                                 .partition_broadcast(P)).then_inc(mb_in, 16)

                def load_e(b, p):
                    W = width(b)
                    sp.dma_start(e_blk[:, bass.ds(p * 2, 2), 0:W],
                                 adj_t[:, bass.ds(p * 2, 2), bass.ds(b * BW, W)]).then_inc(e_in[p], 16)

                def load_x1(b):
                    n = width(b) // P
                    sp.dma_start(out_acc[:, 0:n], x1_t[:, bass.ds(b * IT, n), :]).then_inc(x1_in, 16)

                def store(b):
                    sp.wait_ge(o_out, (b + 1) * H * IT + 2 if not isinstance(b, int) or b < FULL
                               else FULL * H * IT + H * LASTW // P + 2)
                    if isinstance(b, int) and b == FULL:
                        r0 = FULL * BW
                        sp.dma_start(out[r0:r0 + P, :], out_acc[:, 0]).then_inc(out_st, 16)
                        sp.dma_start(out[r0 + P:N, :], out_acc[0:LASTP, 1]).then_inc(out_st, 16)
                    else:
                        sp.dma_start(out[bass.ds(b * BW, BW), :].rearrange("(t p) d -> p t d", p=P),
                                     out_acc[:, 0:IT]).then_inc(out_st, 16)

                load_max(0)
                load_u(0, 0)
                for p in range(PAIRS):
                    load_e(0, p)
                for h in range(1, H):
                    load_u(0, h)
                load_x1(0)

                def body(b):
                    if not isinstance(b, int) or b < FULL:
                        nxt = b + 1
                        for h in range(H - 1):
                            sp.wait_ge(p_ready, (b * H + h + 1) * PAIRS)
                            load_u(nxt, h)
                        sp.wait_ge(e_sub, (b + 1) * NT)
                        load_max(nxt)

                        for p in range(PAIRS):
                            sp.wait_ge(p_ready, (b * H + H - 1) * PAIRS + p + 1)
                            load_e(nxt, p)
                        sp.wait_ge(p_ready, (b + 1) * H * PAIRS)
                        load_u(nxt, H - 1)
                    store(b)
                    if not isinstance(b, int) or b < FULL:
                        sp.wait_ge(out_st, (b + 1) * 16)
                        load_x1(nxt)
                    else:
                        sp.wait_ge(out_st, (FULL + 2) * 16)

                blocks(sp, body)

            @block.gpsimd
            def _(pool):
                def body(b):
                    for p in range(PAIRS):
                        pool.wait_ge(e_in[p], (b + 1) * 16)
                        pool.wait_ge(mb_in, (b + 1) * 16)
                        nc.gpsimd.tensor_tensor(ticks[:, p:p + 1], ones32[:], ones32[:], ALU.add).then_inc(e_here, 1)

                blocks(pool, body)

            @block.scalar
            def _(act):
                def exp_e(b, p):
                    W = width(b)
                    act.wait_ge(e_sub, b * NT + p * 2 + 2)
                    e = e_blk[:, bass.ds(p * 2, 2), 0:W]
                    nc.scalar.activation(e, e, ACT.Exp).then_inc(e_ready, 1)

                def t1(b, h, p):
                    W = width(b)
                    g = (b * H + h) * PAIRS + p
                    if isinstance(p, int) and p == 0:
                        act.wait_ge(u_in[h], (b + 1) * 16)
                    act.wait_ge(acc_done, g + 1)
                    for u in range(2):
                        nc.scalar.activation(t_ring[:, g % T_RING, u, 0:W], u_bc[:, h, 0, 0:W], ACT.Copy,
                                             scale=vv4[:, 0, h, bass.ds(p * 2 + u, 1)]).then_inc(t1_ready, 1)

                def step(b, h, p, after=None):
                    W = width(b)
                    g = (b * H + h) * PAIRS + p
                    after = after or ((b, h, p + 1) if not isinstance(p, int) or p < PAIRS - 1 else None)
                    if after:
                        t1(*after)
                    if e_of(b, h, p):
                        exp_e(*e_of(b, h, p))
                    act.wait_ge(hl_free, g + 1)
                    act.wait_ge(p_ready, g + 1)
                    nc.scalar.activation(hl_ring[:, g % HL_RING, 0, :, 0:W], t_ring[:, g % T_RING, :, 0:W],
                                         ACT.Copy).then_inc(hi_ready, 1)

                def evacuate(b, h):
                    W = width(b)
                    q = b * H + h
                    act.wait_ge(o_done, o_before(b, h) + 1)
                    for k in range(KT):
                        if k < KT - 1:
                            act.wait_ge(z_bank, q * (KT - 1) + k + 1)
                        else:
                            act.wait_ge(hl_free, (q + 1) * PAIRS + HL_RING)
                        nc.scalar.activation(z16[:, 0, k, 0:W], z_ps[:, k, 0:W], ACT.Copy,
                                             scale=ZS).then_inc(z_hi, 1)

                def segment(b, h):
                    nxt = seg_next(b, h)
                    for p in range(2, LOOP0):
                        step(b, h, p)
                    with act.Fori(LOOP0, LOOP1) as p:
                        step(b, h, p)
                    for p in range(LOOP1, PAIRS - 1):
                        step(b, h, p)
                    step(b, h, PAIRS - 1, after=nxt and (*nxt, 0))
                    if nxt:
                        for p in range(2):
                            step(*nxt, p)
                    evacuate(b, h)

                exp_e(0, 0)
                t1(0, 0, 0)
                for p in range(2):
                    step(0, 0, p)

                def body(b):
                    for h in range(H):
                        segment(b, h)

                blocks(act, body, first=1)

            @block.vector
            def _(dve):
                nc.vector.memset(credits[:, 6:7], 0.0).then_inc(acc_done, T_RING)
                nc.vector.memset(credits[:, 7:8], 0.0).then_inc(hl_free, HL_RING)
                nc.vector.memset(credits[:, 8:9], 0.0).then_inc(rs_ps, 2)
                nc.vector.memset(credits[:, 9:10], 0.0).then_inc(rs_sb, 1)
                nc.vector.memset(credits[:, 10:11], 0.0).then_inc(o_done, 1)
                nc.vector.memset(credits[:, 11:12], 0.0).then_inc(o_out, 2)

                def lo_part(b, h, p):
                    W = width(b)
                    g = (b * H + h) * PAIRS + p
                    dve.wait_ge(hi_ready, g + 1)
                    nc.vector.tensor_tensor(hl_ring[:, g % HL_RING, 1, :, 0:W], t_ring[:, g % T_RING, :, 0:W],
                                            hl_ring[:, g % HL_RING, 0, :, 0:W], ALU.subtract).then_inc(lo_ready, 1)

                def accumulate(b, h, p):
                    W = width(b)
                    q = b * H + h
                    g = q * PAIRS + p
                    tp = t_ring[:, g % T_RING, :, 0:W]
                    acc = p_acc[:, h % 2, :, 0:W]
                    if isinstance(p, int) and p == 0:
                        dve.wait_ge(rs_ps, q + 1)
                        nc.vector.tensor_scalar(acc, tp, 1.0, None, ALU.mult).then_inc(acc_done, 1)
                    else:
                        dve.wait_ge(acc_done, g + T_RING)
                        nc.vector.tensor_tensor(acc, acc, tp, ALU.add).then_inc(acc_done, 1)

                def subtract_max(b, p):
                    W = width(b)
                    dve.wait_ge(e_here, b * PAIRS + p + 1)
                    for u in range(2):
                        e = e_blk[:, p * 2 + u, 0:W]
                        nc.vector.tensor_tensor(e, e, max_bc[:, 0:W], ALU.subtract).then_inc(e_sub, 1)

                def step(b, h, p, before=None):
                    W = width(b)
                    g = (b * H + h) * PAIRS + p
                    before = before or ((b, h, p - 1) if not isinstance(p, int) or p > 0 else None)
                    tp = t_ring[:, g % T_RING, :, 0:W]
                    for u in range(2):
                        dve.wait_ge(t1_ready, g * 2 + u + 1)
                        tu = t_ring[:, g % T_RING, u, 0:W]
                        nc.vector.scalar_tensor_tensor(out=tu, in0=u_bc[:, h, 1, 0:W],
                                                       scalar=vv4[:, 1, h, bass.ds(p * 2 + u, 1)], in1=tu,
                                                       op0=ALU.mult, op1=ALU.max).then_inc(stt_done, 1)
                    if before:
                        lo_part(*before)
                    if e_of(b, h, p):
                        subtract_max(*e_of(b, h, p))
                    dve.wait_ge(stt_done, g * 2 + 2)
                    if h == 0:
                        dve.wait_ge(e_ready, b * PAIRS + p + 1)
                    nc.vector.tensor_tensor(tp, tp, e_blk[:, bass.ds(p * 2, 2), 0:W], ALU.mult).then_inc(p_ready, 1)
                    if before:
                        accumulate(*before)

                def evacuate_z(b, h):
                    W = width(b)
                    q = b * H + h
                    for k in range(KT):
                        dve.wait_ge(z_hi, q * KT + k + 1)
                        nc.vector.scalar_tensor_tensor(out=z16[:, 1, k, 0:W], in0=z_ps[:, k, 0:W], scalar=ZS,
                                                       in1=z16[:, 0, k, 0:W], op0=ALU.mult,
                                                       op1=ALU.subtract).then_inc(z_lo, 1)

                def row_factors(b, h):
                    q = b * H + h
                    n = width(b) // P
                    dve.wait_ge(rs_ps, q + 3)
                    nc.vector.reciprocal(rinv[:, 0:n], c_ps[:, 0:n]).then_inc(rinv_done, 1)
                    dve.wait_ge(rinv_done, q + 1)
                    nc.vector.tensor_scalar(rcoef[:, 0:n], rinv[:, 0:n], coef0[:], None,
                                            ALU.mult).then_inc(rs_sb, 1)
                    dve.wait_ge(rs_sb, q + 2)
                    if h == 0:
                        dve.wait_ge(x1_in, (b + 1) * 16)

                def add_out(b, h, its):
                    n = width(b) // P
                    for it in its:
                        f = o_before(b, h) + it
                        dve.wait_ge(o_done, f + 2)
                        if h > 0:
                            dve.wait_ge(o_out, f - n + 3)
                        nc.vector.scalar_tensor_tensor(out=out_acc[:, it], in0=o_ps[:, it % 3],
                                                       scalar=rcoef[:, it:it + 1], in1=out_acc[:, it],
                                                       op0=ALU.mult, op1=ALU.add).then_inc(o_out, 1)

                def segment(b, h):
                    for p in range(4, LOOP0):
                        step(b, h, p)
                    with dve.Fori(LOOP0, LOOP1) as p:
                        step(b, h, p)
                    for p in range(LOOP1, PAIRS):
                        step(b, h, p)
                    last = (b, h, PAIRS - 1)
                    nxt = seg_next(b, h)
                    if nxt:
                        step(*nxt, 0, before=last)
                        step(*nxt, 1)
                    else:
                        lo_part(*last)
                        dve.wait_ge(p_ready, (b * H + H) * PAIRS)
                        accumulate(*last)
                    evacuate_z(b, h)
                    if nxt:
                        step(*nxt, 2)
                    row_factors(b, h)
                    add_out(b, h, [0])
                    if nxt:
                        step(*nxt, 3)
                    add_out(b, h, range(1, width(b) // P))

                subtract_max(0, 0)
                for p in range(4):
                    step(0, 0, p)

                def body(b):
                    for h in range(H):
                        segment(b, h)

                blocks(dve, body, first=1)

            @block.tensor
            def _(pe):
                def pair(b, h, p, first=False, last=False, before=None):
                    W = width(b)
                    g = (b * H + h) * PAIRS + p
                    r = g % HL_RING
                    pe.wait_ge(lo_ready, g + 1)
                    for k in range(KT):
                        if before is not None:
                            pe.wait_ge(z_lo, before * KT + k + 1)
                        for u in range(2):
                            hk = [h16[:, s, p * 2 + u, k * P:(k + 1) * P] for s in range(2)]
                            for n, (hs, ps) in enumerate(((0, 0), (0, 1), (1, 0))):
                                mm = nc.tensor.matmul(z_ps[:, k, 0:W], hk[hs], hl_ring[:, r, ps, u, 0:W],
                                                      start=first and u == 0 and n == 0,
                                                      stop=last and u == 1 and n == 2)
                        if k == KT - 1:
                            mm.then_inc(hl_free, 1)
                        elif last:
                            mm.then_inc(z_bank, 1)

                def project(b, h):
                    W = width(b)
                    n = W // P
                    q = b * H + h
                    pe.wait_ge(acc_done, (q + 1) * PAIRS + T_RING)
                    pe.wait_ge(rs_sb, q + 1)
                    for it in range(n):
                        for u in range(2):
                            mm = nc.tensor.matmul(c_ps[:, it:it + 1], p_acc[:, h % 2, u, it * P:(it + 1) * P],
                                                  ones32[:], start=u == 0, stop=u == 1)
                    mm.then_inc(rs_ps, 1)
                    pe.wait_ge(z_lo, (q + 1) * KT)
                    for it in range(n):
                        pe.wait_ge(o_out, o_before(b, h) + 2 + (it >= 3))
                        for k in range(KT):
                            for m, (zs, ws) in enumerate(((0, 0), (0, 1), (1, 0))):
                                mm = nc.tensor.matmul(o_ps[:, it % 3], z16[:, zs, k, it * P:(it + 1) * P],
                                                      w16[:, k, h, ws], start=k == 0 and m == 0,
                                                      stop=k == KT - 1 and m == 2)
                        mm.then_inc(o_done, 1)

                def segment(b, h):
                    with pe.Fori(1, PAIRS - 1) as p:
                        pair(b, h, p)
                    pair(b, h, PAIRS - 1, last=True)
                    nxt = seg_next(b, h)
                    if nxt:
                        pair(*nxt, 0, first=True, before=b * H + h)
                    project(b, h)

                pair(0, 0, 0, first=True)

                def body(b):
                    for h in range(H):
                        segment(b, h)

                blocks(pe, body)


def kernel(x, adj, L0_gnn_W, L0_gnn_b, L1_gnn_W, L1_gnn_a):
    import numpy as np
    import concourse.bacc as bacc
    from concourse.bass_utils import run_bass_kernel_spmd

    x, adj = np.asarray(x), np.asarray(adj)
    adjT = adj.T
    adjT = np.concatenate([adjT, adjT[:, N - 1:]], axis=1)
    adjT = np.ascontiguousarray(np.concatenate([adjT, adjT[N - 1:]], axis=0))
    arrays = {
        "x_in": np.ascontiguousarray(np.concatenate([x, x[N - 1:]], axis=0)),
        "adjT_in": adjT,
        "W0_in": np.ascontiguousarray(L0_gnn_W),
        "b0_in": np.ascontiguousarray(L0_gnn_b),
        "W1_in": np.ascontiguousarray(L1_gnn_W),
        "a1_in": np.ascontiguousarray(L1_gnn_a),
    }
    nc = bacc.Bacc("TRN2", target_bir_lowering=False, num_devices=1)
    args = [nc.dram_tensor(name, a.shape, mybir.dt.from_np(a.dtype), kind="ExternalInput").ap()
            for name, a in arrays.items()]
    out = nc.dram_tensor("out_dram", (N, D), F32, kind="ExternalOutput").ap()
    gnn_kernel(nc, *args, out)
    result = run_bass_kernel_spmd(nc, [arrays], core_ids=[0])
    return result.results[0]["out_dram"]
```

```python
from contextlib import ExitStack

import concourse.bass as bass
from concourse import mybir

F32 = mybir.dt.float32
F16 = mybir.dt.float16
ALU = mybir.AluOpType
ACT = mybir.ActivationFunctionType
AX_X = mybir.AxisListType.X
RMAX = bass.bass_isa.ReduceOp.max

N = 3327
P = 128
NT = (N + P - 1) // P
NP = NT * P
LASTP = N - (NT - 1) * P
D = 512
KT = D // P
H = 4
PAIRS = NT // 2
BW = 512
NB = (NP + BW - 1) // BW
FULL = NP // BW
LASTW = NP - FULL * BW
IT = BW // P
EPS = 1e-5
SLOPE = 0.01
HS = 2.0 ** 11
PS = 2.0 ** 15
ZS = 2.0 ** -27
WS = 2.0 ** 15
SS = 2.0 ** -12
COEF0 = 1.0 / (SS * HS * WS)
COEF = 1.0 / (ZS * HS * WS * H)
TINY = 1e-30
LOWEST = -3.0e38

ADJ_RING = 4
SEAM_SLOT = 1
A_RING = 2
T_RING = 3
HL_RING = 3


def width(b):
    return BW if not isinstance(b, int) or b < FULL else LASTW


def adj_slot(p):
    return p % ADJ_RING if p < PAIRS - 1 else SEAM_SLOT


def gnn_kernel(nc, x, adjT, W0, b0, W1, a1, out):
    x1_dram = nc.dram_tensor("x1_dram", (NP, D), F32, kind="Internal").ap()
    rows_dram = nc.dram_tensor("rows_dram", (2 * H + 1, NP), F32, kind="Internal").ap()
    x_t = x.rearrange("(t p) d -> p t d", p=P)
    x1_t = x1_dram.rearrange("(t p) d -> p t d", p=P)
    adj_t = adjT.rearrange("(t p) i -> p t i", p=P)

    with ExitStack() as ctx:
        def sb(name, size, dt):
            return ctx.enter_context(nc.sbuf_tensor(name, [P, size], dt))

        def sem(name):
            return ctx.enter_context(nc.semaphore(name))

        h_reg = sb("h_reg", 2 * NT * D, F16)
        x_reg = sb("x_reg", NT * BW, F32)
        w_reg = sb("w_reg", 2 * KT * H * D, F16)
        ring_reg = sb("ring_reg", 8 * BW, F32)
        z_reg = sb("z_reg", 2 * KT * BW, F16)
        t_reg = sb("t_reg", 2 * T_RING * BW, F32)
        hl_reg = sb("hl_reg", HL_RING * 4 * BW, F16)
        ao_reg = sb("ao_reg", 8 * BW, F32)
        row_reg = sb("row_reg", BW, F32)

        h16 = h_reg[:].rearrange("p (s t d) -> p s t d", s=2, t=NT)
        xs = x_reg[:].rearrange("p (t d) -> p t d", t=NT)
        e_blk = xs
        w16 = w_reg[:].rearrange("p (k h s n) -> p k h s n", k=KT, h=H, s=2)
        w_raw = w_reg[:].bitcast(F32).rearrange("p (k h n) -> p k h n", k=KT, h=H)
        w_scaled = hl_reg[:, NP + 2 * BW:NP + 4 * BW].bitcast(F32)
        a_bc = xs[:, 4 * IT:4 * IT + 2 * H]
        adj_ring = ring_reg[:].rearrange("p (s u i) -> p s u i", s=ADJ_RING, u=2)
        a_ring = t_reg[:, 0:2 * BW].bitcast(F16).rearrange("p (s u i) -> p s u i", s=A_RING, u=2)
        w0_raw = w_raw[:, KT - 1]
        w0_16 = t_reg[:, 2 * BW:6 * BW].bitcast(F16).rearrange("p (s k n) -> p s k n", s=2, k=KT)
        s0_16 = z_reg[:].rearrange("p (s k i) -> p s k i", s=2, k=KT)
        adj_max = ao_reg[:, 0:NP]
        adj_cnt = hl_reg[:, 0:NP]
        b0_bc = row_reg[:]
        x_ring = t_reg[:].rearrange("p (s u d) -> p s u d", s=3, u=2)
        ln1_stage = ring_reg[:].rearrange("p (s u d) -> p s u d", s=4, u=2)
        ht_ring = hl_reg[:].bitcast(F32).rearrange("p (s k i) -> p s k i", s=6, k=KT)
        u_bc = ring_reg[:].rearrange("p (h q i) -> p h q i", h=H, q=2)
        z16 = z_reg[:].rearrange("p (s k i) -> p s k i", s=2, k=KT)
        t_ring = x_ring
        hl_ring = hl_reg[:].rearrange("p (r s u i) -> p r s u i", r=HL_RING, s=2, u=2)
        p_acc = ao_reg[:, 0:4 * BW].rearrange("p (a u i) -> p a u i", a=2, u=2)
        out_acc = ao_reg[:, 4 * BW:8 * BW].rearrange("p (t d) -> p t d", t=IT)
        max_bc = row_reg[:]

        ident = sb("ident", P, F32)
        ones32 = sb("ones32", 1, F32)
        ones16 = sb("ones16", 1, F16)
        valid = sb("valid", NT, F32)
        invalid = sb("invalid", 1, F32)
        junk = hl_reg[:, NP:NP + 2 * BW].rearrange("p (u i) -> p u i", u=2)
        credits = sb("credits", 16, F32)
        ticks = sb("ticks", PAIRS, F32)
        bst = sb("bst", NT * 6, F32)
        mv = sb("mv", NT * 2, F32)
        ve = sb("ve", NT, F32)
        sd = sb("sd", NT, F32)
        y0 = sb("y0", NT, F32)
        y1 = sb("y1", NT, F32)
        rs = sb("rs", NT, F32)
        nb = sb("nb", NT, F32)
        wa = sb("wa", KT * 2 * H, F32)
        wmx = ao_reg[:, 4 * BW * 2 - KT * H:]
        wmx1 = sb("wmx1", 1, F32)
        wmax = sb("wmax", 1, F32)
        wsc = sb("wsc", 1, F32)
        coef0 = sb("coef0", 1, F32)
        w0mx = sb("w0mx", 1, F32)
        w0max = sb("w0max", 1, F32)
        w0sc = sb("w0sc", 1, F32)
        w0coef = sb("w0coef", 1, F32)
        degp = sb("degp", NT * NB, F32)
        deg = sb("deg", NT, F32)
        rdeg = sb("rdeg", NT, F32)
        cnt_col = sb("cnt_col", IT, F32)
        sdc = ao_reg[:, NP:NP + NT * 2 * H]
        dmx = sb("dmx", 2 * H, F32)
        dall = sb("dall", 2 * H, F32)
        dn = ao_reg[:, NP + NT * 2 * H:NP + NT * 3 * H]
        vv = sb("vv", 2 * H * NT, F32)
        qq = ao_reg[:, NP + NT * 3 * H:NP + NT * 4 * H]
        lk = ao_reg[:, NP + NT * 4 * H:NP + NT * 5 * H]
        rows = sb("rows", (2 * H + 1) * NT, F32)
        rinv = sb("rinv", 2 * IT, F32)
        rcoef = sb("rcoef", IT, F32)

        mv3 = mv[:].rearrange("p (t c) -> p t c", c=2)
        bst3 = bst[:].rearrange("p (t c) -> p t c", c=6)
        wa3 = wa[:].rearrange("p (k r) -> p k r", k=KT)
        degp3 = degp[:].rearrange("p (t b) -> p t b", b=NB)
        sdc3 = sdc.rearrange("p (t r) -> p t r", r=2 * H)
        sdc4 = sdc.rearrange("p (t h r) -> p h r t", h=H, r=2)
        dn3 = dn.rearrange("p (h t) -> p h t", h=H)
        qq3 = qq.rearrange("p (h t) -> p h t", h=H)
        lk3 = lk.rearrange("p (h t) -> p h t", h=H)
        vv4 = vv[:].rearrange("p (q h t) -> p q h t", q=2, h=H)
        rows3 = rows[:].rearrange("p (r t) -> p r t", t=NT)
        uu4 = rows[:, 0:2 * H * NT].rearrange("p (h r t) -> p h r t", h=H, r=2)

        z_ps = ctx.enter_context(nc.psum_tensor("z_ps", [P, KT, 512], F32))
        o_ps = ctx.enter_context(nc.psum_tensor("o_ps", [P, 3, 512], F32))
        c_ps = ctx.enter_context(nc.psum_tensor("c_ps", [P, 512], F32))

        s_var = sem("s_var")
        s_sqrt = sem("s_sqrt")
        s_ln = sem("s_ln")
        dve_step = sem("dve_step")
        steps = [0]

        def link(dve, ins):
            steps[0] += 1
            ins.then_inc(dve_step, 1)
            dve.wait_ge(dve_step, steps[0])

        def ln_stats(dve, t0, t1, written, count):
            dve.wait_ge(written, t1)
            for t in range(t0, t1):
                nc.vector.bn_aggr(mv3[:, t], bst3[:, t]).then_inc(count, 1)
            dve.wait_ge(count, t1)
            nc.vector.tensor_scalar(ve[:, t0:t1], mv3[:, t0:t1, 1], EPS, None, ALU.add).then_inc(s_var, 1)

        def ln_scalars(dve, t0, t1, group):
            c = slice(t0, t1)
            dve.wait_ge(s_sqrt, group + 1)
            link(dve, nc.vector.reciprocal(y0[:, c], sd[:, c]))
            link(dve, nc.vector.tensor_tensor(y1[:, c], y0[:, c], y0[:, c], ALU.mult))
            link(dve, nc.vector.tensor_tensor(y1[:, c], y1[:, c], ve[:, c], ALU.mult))
            link(dve, nc.vector.tensor_scalar(y1[:, c], y1[:, c], -0.5, 1.5, ALU.mult, ALU.add))
            link(dve, nc.vector.scalar_tensor_tensor(out=rs[:, c], in0=y1[:, c], scalar=HS, in1=y0[:, c],
                                                     op0=ALU.mult, op1=ALU.mult))
            nc.vector.scalar_tensor_tensor(out=nb[:, c], in0=mv3[:, c, 0], scalar=-1.0, in1=rs[:, c],
                                           op0=ALU.mult, op1=ALU.mult).then_inc(s_ln, 1)

        def ln_sqrt(act, t0, t1, group):
            act.wait_ge(s_var, group + 1)
            nc.scalar.activation(sd[:, t0:t1], ve[:, t0:t1], ACT.Sqrt).then_inc(s_sqrt, 1)

        groups0 = [(0, 2), (2, 4), (4, 8), (8, 14), (14, 20), (20, NT)]
        W0_GROUP = 3
        x_in1 = [sem(f"x_in1_{s}") for s in range(3)]
        x_in = [sem(f"x_in{c}") for c in range(len(groups0))]
        w_in = [sem(f"w_in{k}") for k in range(KT)]
        a_in = sem("a_in")
        s_bst = sem("s_bst")
        s_mv = sem("s_mv")
        s_const = sem("s_const")
        s_fill = sem("s_fill")
        s_ident0 = sem("s_ident0")
        h0_relu = sem("h0_relu")
        h0_hi = sem("h0_hi")
        h0_lo = sem("h0_lo")
        s_wred = sem("s_wred")
        s_wmx = sem("s_wmx")
        s_wmax = sem("s_wmax")
        s_wsc = sem("s_wsc")
        w_step = sem("w_step")
        adj_in = [sem(f"adj_in{s}") for s in range(ADJ_RING)]
        w0_in = sem("w0_in")
        b0_in = sem("b0_in")
        mx_done = sem("mx_done")
        cnt_done = sem("cnt_done")
        a_ready = sem("a_ready")
        a_pe = sem("a_pe")
        a_act = sem("a_act")
        s0_bank = sem("s0_bank")
        s0_hi = sem("s0_hi")
        s0_lo = sem("s0_lo")
        bias_in = sem("bias_in")
        s_w0mx = sem("s_w0mx")
        s_w0max = sem("s_w0max")
        s_w0sc = sem("s_w0sc")
        s_w0hi = sem("s_w0hi")
        s_w0lo = sem("s_w0lo")
        cnt_ps = sem("cnt_ps")
        cnt_sb = sem("cnt_sb")
        o0_done = sem("o0_done")
        o0_out = sem("o0_out")
        MX0 = 2 * (ADJ_RING + 1)

        with nc.Block() as block:
            @block.sync
            def _(sp):
                def load(b, p, slot, turn):
                    W = width(b)
                    g = b * PAIRS + p
                    sp.wait_ge(mx_done, MX0 + 2 * (g - back(slot, turn)) + 2)
                    sp.dma_start(adj_ring[:, slot, :, 0:W],
                                 adj_t[:, bass.ds(p * 2, 2), bass.ds(b * BW, W)]).then_inc(adj_in[slot], 16)

                def back(slot, turn):
                    if isinstance(turn, int) and turn == 0:
                        return SEAM_SLOT + 1 if slot == SEAM_SLOT else ADJ_RING + 1
                    if isinstance(turn, int) and turn == PAIRS // ADJ_RING:
                        return ADJ_RING - SEAM_SLOT
                    return ADJ_RING

                def block_loads(b, first=0):
                    for slot in range(first, ADJ_RING):
                        load(b, slot, slot, 0)
                    with sp.Fori(1, PAIRS // ADJ_RING) as turn:
                        for slot in range(ADJ_RING):
                            load(b, turn * ADJ_RING + slot, slot, turn)
                    load(b, PAIRS - 1, SEAM_SLOT, PAIRS // ADJ_RING)

                def load_x(c):
                    t0, t1 = groups0[c]
                    sp.dma_start(xs[:, t0:t1, :], x_t[:, t0:t1, :]).then_inc(x_in[c], 16)

                load_x(0)
                load_x(1)
                load_x(2)
                for slot in range(3):
                    load(0, slot, slot, 0)
                    load_x(slot + 3)
                load(0, 3, 3, 0)
                sp.dma_start(w0_raw, W0.rearrange("(k p) n -> p k n", p=P)).then_inc(w0_in, 16)
                sp.dma_start(b0_bc, b0.partition_broadcast(P)).then_inc(b0_in, 16)
                block_loads(0, first=ADJ_RING)

                def load_w1(k):
                    sp.dma_start(w_raw[:, k], W1[k * P:(k + 1) * P, :].rearrange("p (h n) -> p h n", h=H)
                                 ).then_inc(w_in[k], 16)

                load(1, 0, 0, 0)
                load_w1(0)
                sp.wait_ge(h0_lo, PAIRS)
                sp.dma_start(a_bc, a1.rearrange("h (q c) o -> (h q) (c o)", q=2)
                             .partition_broadcast(P)).then_inc(a_in, 16)
                for slot in range(1, ADJ_RING):
                    load(1, slot, slot, 0)
                load_w1(1)
                block_loads(1, first=ADJ_RING)
                load_w1(2)
                load_w1(3)
                with sp.Fori(2, FULL) as b:
                    block_loads(b)
                block_loads(FULL)
                sp.wait_ge(a_pe, NB * PAIRS + A_RING)
                sp.wait_ge(a_act, 2 * (NB * PAIRS + A_RING))
                sp.wait_ge(cnt_done, NB * NT + 1)
                sp.dma_start(x_ring[:, 0], x_t[:, 0:2, :]).then_inc(x_in1[0], 16)

            @block.gpsimd
            def _(pool):
                nc.gpsimd.memset(ident[:], 0.0).then_inc(s_ident0, 1)
                nc.gpsimd.memset(valid[:], 1.0).then_inc(s_ident0, 1)
                pool.wait_ge(s_ident0, 2)
                nc.gpsimd.affine_select(out=ident[:], in_=ident[:], compare_op=ALU.not_equal, fill=1.0,
                                        base=0, pattern=[[-1, P]], channel_multiplier=1).then_inc(s_const, 1)
                nc.gpsimd.affine_select(out=valid[:, NT - 1:NT], in_=valid[:, NT - 1:NT],
                                        compare_op=ALU.is_ge, fill=0.0, base=LASTP - 1, pattern=[[0, 1]],
                                        channel_multiplier=-1).then_inc(s_const, 1)
                nc.gpsimd.memset(adj_max, LOWEST).then_inc(s_fill, 1)
                nc.gpsimd.memset(adj_cnt.bitcast(F32), 0.0).then_inc(s_fill, 1)
                for p in range(PAIRS):
                    pool.wait_ge(h0_hi, p + 1)
                    nc.gpsimd.tensor_tensor(h16[:, 1, 2 * p:2 * p + 2], xs[:, 2 * p:2 * p + 2],
                                            h16[:, 0, 2 * p:2 * p + 2], ALU.subtract).then_inc(h0_lo, 1)
                    if p == groups0[W0_GROUP + 1][1] // 2 - 1:
                        pool.wait_ge(s_w0mx, 1)
                        nc.gpsimd.partition_all_reduce(w0max[:], w0mx[:], P, RMAX).then_inc(s_w0max, 1)
                pool.wait_ge(s_wmx, 1)
                nc.gpsimd.partition_all_reduce(wmax[:], wmx1[:], P, RMAX).then_inc(s_wmax, 1)
                pool.wait_ge(s_wsc, 1)
                for n in range(KT * H):
                    k, h = n // H, n % H
                    if n > 0:
                        pool.wait_ge(w_step, 3 * n)
                    nc.gpsimd.tensor_scalar(w_scaled, w_raw[:, k, h], wsc[:], None, ALU.mult).then_inc(w_step, 1)
                    pool.wait_ge(w_step, 3 * n + 1)
                    nc.gpsimd.tensor_copy(w16[:, k, h, 0], w_scaled).then_inc(w_step, 1)
                    pool.wait_ge(w_step, 3 * n + 2)
                    nc.gpsimd.tensor_tensor(w16[:, k, h, 1], w_scaled, w16[:, k, h, 0],
                                            ALU.subtract).then_inc(w_step, 1)

            @block.vector
            def _(dve):
                nc.vector.memset(ones32[:], 1.0)
                nc.vector.memset(ones16[:], 1.0).then_inc(a_pe, A_RING)
                nc.vector.memset(credits[:, 1:2], 0.0).then_inc(a_act, 2 * A_RING)
                nc.vector.memset(credits[:, 3:4], 0.0).then_inc(cnt_sb, 1)
                nc.vector.memset(credits[:, 4:5], 0.0).then_inc(o0_out, 2)
                nc.vector.memset(credits[:, 5:6], 0.0).then_inc(o0_done, 1)
                nc.vector.memset(credits[:, 6:7], 0.0).then_inc(cnt_done, 1)
                nc.vector.memset(credits[:, 7:8], 0.0).then_inc(mx_done, MX0)

                def pair(b, p, slot, turn):
                    W = width(b)
                    g = b * PAIRS + p
                    cols = bass.ds(b * BW, W)
                    dve.wait_ge(adj_in[slot], (b * (PAIRS // ADJ_RING + (slot == SEAM_SLOT)) + turn + 1) * 16)
                    dve.wait_ge(a_pe, g + 1)
                    dve.wait_ge(a_act, g * 2 + 2)
                    for u in range(2):
                        nc.vector.tensor_scalar(a_ring[:, g % A_RING, u, 0:W], adj_ring[:, slot, u, 0:W], 0.0,
                                                valid[:, bass.ds(p * 2 + u, 1)], ALU.not_equal,
                                                ALU.mult).then_inc(a_ready, 1)
                    for u in range(2):
                        dve.wait_ge(mx_done, g * 2 + MX0 + u)
                        nc.vector.tensor_tensor(adj_max[:, cols], adj_max[:, cols], adj_ring[:, slot, u, 0:W],
                                                ALU.max).then_inc(mx_done, 1)
                        dve.wait_ge(a_ready, g * 2 + u + 1)
                        dve.wait_ge(cnt_done, g * 2 + u + 1)
                        nc.vector.tensor_tensor(adj_cnt[:, cols], adj_cnt[:, cols], a_ring[:, g % A_RING, u, 0:W],
                                                ALU.add).then_inc(cnt_done, 1)

                def s0_lo_part(b):
                    W = width(b)
                    for k in range(KT):
                        dve.wait_ge(s0_hi, b * KT + k + 1)
                        nc.vector.scalar_tensor_tensor(out=s0_16[:, 1, k, 0:W], in0=z_ps[:, k, 0:W], scalar=SS,
                                                       in1=s0_16[:, 0, k, 0:W], op0=ALU.mult,
                                                       op1=ALU.subtract).then_inc(s0_lo, 1)

                def head(b):
                    pair(b, 0, 0, 0)
                    s0_lo_part(b - 1)
                    pair(b, 1, 1, 0)
                    pair(b, 2, 2, 0)

                def rest(b):
                    pair(b, 3, 3, 0)
                    with dve.Fori(1, PAIRS // ADJ_RING) as turn:
                        for slot in range(ADJ_RING):
                            pair(b, turn * ADJ_RING + slot, slot, turn)
                    pair(b, PAIRS - 1, SEAM_SLOT, PAIRS // ADJ_RING)

                def evacuate(b, chunks=()):
                    W = width(b)
                    n = W // P
                    dve.wait_ge(cnt_ps, b + 1)
                    nc.vector.tensor_copy(cnt_col[:, 0:n], c_ps[:, 0:n]).then_inc(cnt_sb, 1)
                    for it in range(n):
                        f = b * IT + it
                        for c in chunks[it:it + 1]:
                            w1_chunk(c)
                        dve.wait_ge(o0_done, f + 2)
                        dve.wait_ge(bias_in, f + 1)
                        nc.vector.scalar_tensor_tensor(out=xs[:, f], in0=o_ps[:, it % 2], scalar=w0coef[:],
                                                       in1=xs[:, f], op0=ALU.mult, op1=ALU.add).then_inc(o0_out, 1)

                def variance(c):
                    t0, t1 = groups0[c]
                    dve.wait_ge(x_in[c], 16)
                    for t in range(t0, t1):
                        nc.vector.bn_stats(bst3[:, t], xs[:, t]).then_inc(s_bst, 1)
                    ln_stats(dve, t0, t1, s_bst, s_mv)

                def w1_chunk(n):
                    k, h = n // H, n % H
                    if h == 0:
                        dve.wait_ge(w_in[k], 16)
                    nc.vector.tensor_reduce(wmx[:, n:n + 1], w_raw[:, k, h], AX_X, ALU.max,
                                            apply_absolute_value=True).then_inc(s_wred, 1)
                    for r in (2 * h, 2 * h + 1):
                        link(dve, nc.vector.tensor_tensor_reduce(
                            out=w_scaled, in0=w_raw[:, k, h], in1=a_bc[:, r], scale=1.0, scalar=0.0,
                            op0=ALU.mult, op1=ALU.add, accum_out=wa3[:, k, r:r + 1]))

                def w1_scale():
                    dve.wait_ge(s_wmax, 1)
                    link(dve, nc.vector.tensor_scalar(wmax[:], wmax[:], TINY, None, ALU.max))
                    link(dve, nc.vector.reciprocal(wsc[:], wmax[:]))
                    nc.vector.tensor_scalar(coef0[:], wmax[:], COEF, None, ALU.mult)
                    link(dve, nc.vector.tensor_scalar(invalid[:], valid[:, NT - 1:NT], -1.0, 1.0, ALU.mult,
                                                      ALU.add))
                    nc.vector.tensor_scalar(wsc[:], wsc[:], WS, None, ALU.mult).then_inc(s_wsc, 1)

                for c in range(2):
                    variance(c)
                    ln_scalars(dve, *groups0[c], c)
                dve.wait_ge(s_const, 2)
                dve.wait_ge(s_fill, 2)
                for c, (t0, t1) in enumerate(groups0):
                    if c + 2 < len(groups0):
                        variance(c + 2)
                    for p in range(t0 // 2, t1 // 2):
                        pair(0, p, adj_slot(p), p // ADJ_RING)
                    if c + 2 < len(groups0):
                        ln_scalars(dve, *groups0[c + 2], c + 2)
                    if c == W0_GROUP:
                        dve.wait_ge(w0_in, 16)
                        nc.vector.tensor_reduce(w0mx[:], w0_raw.rearrange("p h n -> p (h n)"), AX_X, ALU.max,
                                                apply_absolute_value=True).then_inc(s_w0mx, 1)
                    if c == W0_GROUP + 1:
                        dve.wait_ge(s_w0max, 1)
                        link(dve, nc.vector.tensor_scalar(w0max[:], w0max[:], TINY, None, ALU.max))
                        link(dve, nc.vector.reciprocal(w0sc[:], w0max[:]))
                        nc.vector.tensor_scalar(w0coef[:], w0max[:], COEF0, None, ALU.mult)
                        nc.vector.tensor_scalar(w0sc[:], w0sc[:], WS, None, ALU.mult).then_inc(s_w0sc, 1)
                dve.wait_ge(s_w0hi, 1)
                nc.vector.scalar_tensor_tensor(out=w0_16[:, 1], in0=w0_raw, scalar=w0sc[:], in1=w0_16[:, 0],
                                               op0=ALU.mult, op1=ALU.subtract).then_inc(s_w0lo, 1)
                head(1)
                dve.wait_ge(a_in, 16)
                evacuate(0, chunks=range(0, 4))
                for b in (1, 2):
                    for p in range(3, PAIRS):
                        if p in (4, 6, 8, 10):
                            w1_chunk(b * 8 - 4 + (p - 4) // 2)
                        pair(b, p, adj_slot(p), p // ADJ_RING)
                    head(b + 1)
                    if b == 1:
                        evacuate(b, chunks=range(8, 12))
                dve.wait_ge(s_wred, KT * H)
                nc.vector.tensor_reduce(wmx1[:], wmx, AX_X, ALU.max).then_inc(s_wmx, 1)
                evacuate(2)
                w1_scale()
                with dve.Fori(3, FULL - 1) as b:
                    rest(b)
                    head(b + 1)
                    evacuate(b)
                for b in (FULL - 1, FULL):
                    rest(b)
                    if b < FULL:
                        head(b + 1)
                    else:
                        s0_lo_part(b)
                    evacuate(b)

            @block.scalar
            def _(act):
                def relu(c):
                    t0, t1 = groups0[c]
                    act.wait_ge(s_ln, c + 1)
                    for t in range(t0, t1):
                        nc.scalar.activation(xs[:, t], xs[:, t], ACT.Relu, bias=nb[:, t:t + 1],
                                             scale=rs[:, t:t + 1]).then_inc(h0_relu, 1)
                        if t % 2:
                            act.wait_ge(h0_relu, t + 1)
                            nc.scalar.activation(h16[:, 0, t - 1:t + 1], xs[:, t - 1:t + 1],
                                                 ACT.Copy).then_inc(h0_hi, 1)

                def degrees(b, p):
                    W = width(b)
                    Wv = W if W == BW else W - (NP - N)
                    g = b * PAIRS + p
                    for u in range(2):
                        act.wait_ge(a_ready, g * 2 + u + 1)
                        act.wait_ge(a_act, g * 2 + u + 2 * A_RING - 1)
                        nc.scalar.activation(junk[:, u, 0:Wv], a_ring[:, g % A_RING, u, 0:Wv], ACT.Copy,
                                             accum_out=degp3[:, bass.ds(p * 2 + u, 1), b]).then_inc(a_act, 1)

                def evacuate(b):
                    W = width(b)
                    act.wait_ge(o0_done, b * IT + 1)
                    for k in range(KT):
                        if k < KT - 1:
                            act.wait_ge(s0_bank, b * (KT - 1) + k + 1)
                        else:
                            act.wait_ge(a_pe, (b + 1) * PAIRS + A_RING)
                        nc.scalar.activation(s0_16[:, 0, k, 0:W], z_ps[:, k, 0:W], ACT.Copy,
                                             scale=SS).then_inc(s0_hi, 1)

                def bias(b):
                    act.wait_ge(cnt_sb, b + 2)
                    for it in range(width(b) // P):
                        nc.scalar.activation(xs[:, b * IT + it], b0_bc, ACT.Copy,
                                             scale=cnt_col[:, it:it + 1]).then_inc(bias_in, 1)

                for c in range(2):
                    ln_sqrt(act, *groups0[c], c)
                    relu(c)
                for c, (t0, t1) in enumerate(groups0):
                    if c + 2 < len(groups0):
                        ln_sqrt(act, *groups0[c + 2], c + 2)
                    for p in range(t0 // 2, t1 // 2):
                        degrees(0, p)
                    if c + 2 < len(groups0):
                        relu(c + 2)
                    if c == W0_GROUP + 1:
                        act.wait_ge(s_w0sc, 1)
                        nc.scalar.activation(w0_16[:, 0], w0_raw, ACT.Copy, scale=w0sc[:]).then_inc(s_w0hi, 1)
                evacuate(0)
                act.wait_ge(b0_in, 16)

                def body(b):
                    for p in range(3):
                        degrees(b, p)
                    bias(b - 1)
                    with act.Fori(3, PAIRS) as p:
                        degrees(b, p)
                    evacuate(b)

                with act.Fori(1, FULL) as b:
                    body(b)
                body(FULL)
                bias(FULL)

            @block.tensor
            def _(pe):
                def pair(b, p, first=False, last=False, evacuated=None):
                    W = width(b)
                    g = b * PAIRS + p
                    if isinstance(b, int) and b == 0:
                        pe.wait_ge(h0_lo, p + 1)
                    pe.wait_ge(a_ready, g * 2 + 2)
                    for k in range(KT):
                        if evacuated is not None:
                            pe.wait_ge(s0_lo, evacuated * KT + k + 1)
                        for u in range(2):
                            for s in range(2):
                                mm = nc.tensor.matmul(
                                    z_ps[:, k, 0:W], h16[:, s, p * 2 + u, k * P:(k + 1) * P],
                                    a_ring[:, g % A_RING, u, 0:W], start=first and u == 0 and s == 0,
                                    stop=last and u == 1 and s == 1)
                        if k == KT - 1:
                            mm.then_inc(a_pe, 1)
                        elif last:
                            mm.then_inc(s0_bank, 1)

                def project(b):
                    W = width(b)
                    n = W // P
                    pe.wait_ge(cnt_done, (b + 1) * NT + 1)
                    pe.wait_ge(cnt_sb, b + 1)
                    for it in range(n):
                        mm = nc.tensor.matmul(c_ps[:, it:it + 1], adj_cnt[:, bass.ds(b * BW + it * P, P)], ones16[:],
                                              start=True, stop=True)
                    mm.then_inc(cnt_ps, 1)
                    pe.wait_ge(s0_lo, (b + 1) * KT)
                    if isinstance(b, int) and b == 0:
                        pe.wait_ge(s_w0lo, 1)
                    for it in range(n):
                        f = b * IT + it
                        pe.wait_ge(o0_out, f + 1)
                        for k in range(KT):
                            for m, (zs, ws) in enumerate(((0, 0), (0, 1), (1, 0))):
                                mm = nc.tensor.matmul(o_ps[:, it % 2], s0_16[:, zs, k, it * P:(it + 1) * P],
                                                      w0_16[:, ws, k], start=k == 0 and m == 0,
                                                      stop=k == KT - 1 and m == 2)
                        mm.then_inc(o0_done, 1)

                pair(0, 0, first=True)

                def body(b):
                    with pe.Fori(1, PAIRS - 1) as p:
                        pair(b, p)
                    pair(b, PAIRS - 1, last=True)
                    pair(b + 1, 0, first=True, evacuated=b)
                    project(b)

                body(0)
                with pe.Fori(1, FULL - 1) as b:
                    body(b)
                body(FULL - 1)
                for p in range(1, PAIRS):
                    pair(FULL, p, last=p == PAIRS - 1)
                project(FULL)

        x1_ready = sem("x1_ready")
        x1_bst = sem("x1_bst")
        s_mv1 = sem("s_mv1")
        x1_out = sem("x1_out")
        mt_ps = sem("mt_ps")
        mt_red = sem("mt_red")
        st1_ready = sem("st1_ready")
        st1_split = sem("st1_split")
        hi1_done = sem("hi1_done")
        tr_ps = sem("tr_ps")
        tr_sb = sem("tr_sb")
        sd_ps = sem("sd_ps")
        s_dmx = sem("s_dmx")
        s_dall = sem("s_dall")
        s_dn = sem("s_dn")
        s_vv = sem("s_vv")
        s_uarg = sem("s_uarg")
        s_uexp = sem("s_uexp")
        s_rows = sem("s_rows")
        rt_ps = sem("rt_ps")
        rt_sb = sem("rt_sb")
        rows_out = sem("rows_out")
        u_in = [sem(f"u_in{h}") for h in range(H)]
        e_in = [sem(f"e_in{p}") for p in range(PAIRS)]
        mb_in = sem("mb_in")
        x1_in = sem("x1_in")

        def load_u(sp, b, h):
            W = width(b)
            sp.dma_start(u_bc[:, h, :, 0:W], rows_dram[2 * h:2 * h + 2, bass.ds(b * BW, W)]
                         .partition_broadcast(P)).then_inc(u_in[h], 16)

        def load_max(sp, b):
            W = width(b)
            sp.dma_start(max_bc[:, 0:W], rows_dram[2 * H, bass.ds(b * BW, W)]
                         .partition_broadcast(P)).then_inc(mb_in, 16)

        def load_e(sp, b, p):
            W = width(b)
            sp.dma_start(e_blk[:, bass.ds(p * 2, 2), 0:W],
                         adj_t[:, bass.ds(p * 2, 2), bass.ds(b * BW, W)]).then_inc(e_in[p], 16)

        def load_x1(sp, b):
            n = width(b) // P
            sp.dma_start(out_acc[:, 0:n], x1_t[:, bass.ds(b * IT, n), :]).then_inc(x1_in, 16)

        EARLY = 5
        groups1 = [(0, 2), (2, 4), (4, 8), (8, 14), (14, 20), (20, NT)]
        NR = 2 * H + 1
        RH = NR * NT // 2
        max_groups = [(t, min(t + IT, NT)) for t in range(0, NT, IT)]
        row_stage = row_reg[:, 0:2 * P].rearrange("p (a i) -> p a i", a=2)

        with nc.Block() as block:
            @block.sync
            def _(sp):
                def load(p, slot, turn):
                    if not (isinstance(turn, int) and turn == 0):
                        sp.wait_ge(x1_ready, p * 2 - 4)
                    sp.dma_start(x_ring[:, slot], x_t[:, bass.ds(p * 2, 2), :]).then_inc(x_in1[slot], 16)

                def store(p):
                    sp.wait_ge(x1_ready, p * 2 + 2)
                    sp.dma_start(x1_t[:, bass.ds(p * 2, 2), :], xs[:, bass.ds(p * 2, 2)]).then_inc(x1_out, 16)

                for p in range(1, 3):
                    load(p, p, 0)
                with sp.Fori(1, PAIRS // 3) as turn:
                    for slot in range(3):
                        load(turn * 3 + slot, slot, turn)
                        store(turn * 3 + slot - 3)
                load(PAIRS - 1, 0, PAIRS // 3)
                for p in range(PAIRS - 4, PAIRS):
                    store(p)
                sp.wait_ge(x1_out, 16 * PAIRS)
                sp.wait_ge(st1_ready, NT)
                for p in range(EARLY):
                    load_e(sp, 0, p)
                sp.wait_ge(rt_sb, 2)
                rows_v = rows_dram.rearrange("r (t i) -> (r t) i", i=P)
                for a in range(2):
                    sp.dma_start(rows_v[a * RH:(a + 1) * RH, :], row_stage[0:RH, a]).then_inc(rows_out, 16)
                sp.wait_ge(rows_out, 32)
                load_max(sp, 0)
                load_u(sp, 0, 0)
                for p in range(EARLY, PAIRS):
                    load_e(sp, 0, p)
                for h in range(1, H):
                    load_u(sp, 0, h)
                load_x1(sp, 0)

            @block.gpsimd
            def _(pool):
                for p in range(PAIRS):
                    pool.wait_ge(hi1_done, p + 1)
                    nc.gpsimd.tensor_tensor(h16[:, 1, 2 * p:2 * p + 2], ln1_stage[:, p % 4],
                                            h16[:, 0, 2 * p:2 * p + 2], ALU.subtract).then_inc(st1_split, 1)
                pool.wait_ge(s_dmx, 1)
                nc.gpsimd.partition_all_reduce(dall[:], dmx[:], P, RMAX).then_inc(s_dall, 1)

            @block.scalar
            def _(act):
                def transposed(t):
                    act.wait_ge(tr_ps, t + 1)
                    if t >= 6:
                        act.wait_ge(sd_ps, t - 5)
                    nc.scalar.activation(ht_ring[:, t % 6], o_ps[:, t % 3]
                                         .rearrange("p (k i) -> p k i", k=KT), ACT.Copy).then_inc(tr_sb, 1)

                ln_sqrt(act, *groups1[0], len(groups0))
                for c, (t0, t1) in enumerate(groups1):
                    act.wait_ge(s_ln, len(groups0) + c + 1)
                    for t in range(t0, t1):
                        p = t // 2
                        if t == t1 - 1 and c + 1 < len(groups1):
                            ln_sqrt(act, *groups1[c + 1], len(groups0) + c + 1)
                        if t % 2 == 0 and p >= 4:
                            act.wait_ge(st1_split, p - 3)
                            act.wait_ge(tr_ps, 2 * (p - 3))
                        nc.scalar.activation(ln1_stage[:, p % 4, t % 2], xs[:, t], ACT.Relu, bias=nb[:, t:t + 1],
                                             scale=rs[:, t:t + 1]).then_inc(st1_ready, 1)
                        if t % 2:
                            act.wait_ge(st1_ready, t + 1)
                            nc.scalar.activation(h16[:, 0, t - 1:t + 1], ln1_stage[:, p % 4],
                                                 ACT.Copy).then_inc(hi1_done, 1)
                        if t > 0:
                            transposed(t - 1)
                transposed(NT - 1)
                act.wait_ge(s_dn, 1)
                for q, f in ((0, 1.0), (1, SLOPE)):
                    nc.scalar.activation(vv4[:, q], dn3, ACT.Exp, scale=f).then_inc(s_vv, 1)
                act.wait_ge(s_uarg, 2)
                nc.scalar.activation(rows[:, 0:2 * H * NT], rows[:, 0:2 * H * NT], ACT.Exp).then_inc(s_uexp, 1)
                for a in range(2):
                    act.wait_ge(rt_ps, a + 1)
                    nc.scalar.activation(row_stage[0:RH, a], o_ps[0:RH, a, 0:P], ACT.Copy).then_inc(rt_sb, 1)

            @block.tensor
            def _(pe):
                def transpose_max(n):
                    t0, t1 = max_groups[n]
                    if n >= KT:
                        pe.wait_ge(mt_red, n - KT + 1)
                    for t in range(t0, t1):
                        mm = nc.tensor.transpose(z_ps[:, n % KT, (t - t0) * P:(t - t0 + 1) * P],
                                                 adj_max[:, t * P:(t + 1) * P], ident[:])
                    mm.then_inc(mt_ps, 1)

                for n in range(KT):
                    transpose_max(n)

                def scores(t):
                    pe.wait_ge(tr_sb, t + 1)
                    for k in range(KT):
                        mm = nc.tensor.matmul(c_ps[:, t * 2 * H:(t + 1) * 2 * H], ht_ring[:, t % 6, k], wa3[:, k],
                                              start=k == 0, stop=k == KT - 1)
                    mm.then_inc(sd_ps, 1)

                for t in range(NT):
                    pe.wait_ge(st1_ready, t + 1)
                    if t >= 3:
                        pe.wait_ge(tr_sb, t - 2)
                    for k in range(KT):
                        mm = nc.tensor.transpose(o_ps[:, t % 3, k * P:(k + 1) * P],
                                                 ln1_stage[:, (t // 2) % 4, t % 2, k * P:(k + 1) * P], ident[:])
                    mm.then_inc(tr_ps, 1)
                    if t >= 1:
                        scores(t - 1)
                    if t == NT - 6:
                        for n in range(KT, len(max_groups)):
                            transpose_max(n)
                scores(NT - 1)
                pe.wait_ge(s_rows, 1)
                pe.wait_ge(tr_sb, NT)
                for a in range(2):
                    nc.tensor.transpose(o_ps[0:RH, a, 0:P], rows[:, a * RH:(a + 1) * RH],
                                        ident[:]).then_inc(rt_ps, 1)

            @block.vector
            def _(dve):
                link(dve, nc.vector.tensor_reduce(deg[:], degp3, AX_X, ALU.add))
                link(dve, nc.vector.tensor_tensor(deg[:, NT - 1:NT], deg[:, NT - 1:NT], invalid[:], ALU.add))
                link(dve, nc.vector.reciprocal(rdeg[:], deg[:]))

                def x1_pair(p, slot, turn):
                    dve.wait_ge(x_in1[slot], (turn + 1) * 16)
                    for u in range(2):
                        t = p * 2 + u
                        nc.vector.scalar_tensor_tensor(out=xs[:, t], in0=xs[:, t], scalar=rdeg[:, bass.ds(t, 1)],
                                                       in1=x_ring[:, slot, u], op0=ALU.mult,
                                                       op1=ALU.add).then_inc(x1_ready, 1)
                    for u in range(2):
                        t = p * 2 + u
                        dve.wait_ge(x1_ready, t + 1)
                        nc.vector.bn_stats(bst3[:, t], xs[:, t]).then_inc(x1_bst, 1)

                def reduce_max(n):
                    t0, t1 = max_groups[n]
                    dve.wait_ge(mt_ps, n + 1)
                    nc.vector.tensor_reduce(rows3[:, 2 * H, t0:t1],
                                            z_ps[:, n % KT, 0:(t1 - t0) * P].rearrange("p (t i) -> p t i", i=P),
                                            AX_X, ALU.max).then_inc(mt_red, 1)

                for c, (t0, t1) in enumerate(groups1):
                    for p in range(t0 // 2, t1 // 2):
                        x1_pair(p, p % 3, p // 3)
                    ln_stats(dve, t0, t1, x1_bst, s_mv1)
                    ln_scalars(dve, t0, t1, len(groups0) + c)
                    if c == 3:
                        for n in range(KT):
                            reduce_max(n)
                for n in range(KT, len(max_groups)):
                    reduce_max(n)
                dve.wait_ge(sd_ps, NT)
                link(dve, nc.vector.tensor_scalar(sdc, c_ps[:, 0:NT * 2 * H], 1.0 / HS, None, ALU.mult))
                nc.vector.tensor_reduce(dmx[:], sdc.rearrange("p (t r) -> p r t", r=2 * H), AX_X,
                                        ALU.max).then_inc(s_dmx, 1)
                dve.wait_ge(s_dall, 1)
                dh = dall[:].rearrange("p (h r) -> p h r", r=2)[:, :, 1:2].broadcast_to((P, H, NT))
                nc.vector.tensor_tensor(dn3, sdc4[:, :, 1], dh, ALU.subtract).then_inc(s_dn, 1)
                link(dve, nc.vector.tensor_tensor(qq3, sdc4[:, :, 0], dh, ALU.add))
                link(dve, nc.vector.scalar_tensor_tensor(out=lk3, in0=qq3, scalar=SLOPE, in1=qq3,
                                                         op0=ALU.mult, op1=ALU.max))
                nc.vector.tensor_tensor(uu4[:, :, 0], qq3, lk3, ALU.subtract).then_inc(s_uarg, 1)
                nc.vector.scalar_tensor_tensor(out=uu4[:, :, 1], in0=qq3, scalar=SLOPE, in1=lk3,
                                               op0=ALU.mult, op1=ALU.subtract).then_inc(s_uarg, 1)
                dve.wait_ge(s_vv, 2)
                link(dve, nc.vector.tensor_scalar(vv[:].rearrange("p (r t) -> p r t", t=NT)[:, :, NT - 1],
                                                  vv[:].rearrange("p (r t) -> p r t", t=NT)[:, :, NT - 1],
                                                  valid[:, NT - 1:NT], None, ALU.mult))
                dve.wait_ge(s_uexp, 1)
                nc.vector.tensor_scalar(rows[:, 0:2 * H * NT], rows[:, 0:2 * H * NT], PS, None,
                                        ALU.mult).then_inc(s_rows, 1)

        out_st = sem("out_st")
        e_here = sem("e_here")
        e_sub = sem("e_sub")
        e_ready = sem("e_ready")
        t1_ready = sem("t1_ready")
        stt_done = sem("stt_done")
        p_ready = sem("p_ready")
        acc_done = sem("acc_done")
        hi_ready = sem("hi_ready")
        lo_ready = sem("lo_ready")
        hl_free = sem("hl_free")
        z_bank = sem("z_bank")
        z_hi = sem("z_hi")
        z_lo = sem("z_lo")
        acc_sum = sem("acc_sum")
        rs_ps = sem("rs_ps")
        rs_sb = sem("rs_sb")
        rinv_done = sem("rinv_done")
        o_done = sem("o_done")
        o_out = sem("o_out")
        LOOP0, LOOP1 = 5, PAIRS - 2
        E_LATE = PAIRS - LOOP1
        assert LOOP1 - LOOP0 + (LOOP1 - LOOP0 + 1) == PAIRS

        def seg_next(b, h):
            return (b, h + 1) if h < H - 1 else ((b + 1, 0) if not isinstance(b, int) or b < FULL else None)

        def o_before(b, h):
            if isinstance(b, int) and b == FULL:
                return FULL * H * IT + h * (LASTW // P)
            return (b * H + h) * IT

        def e_of(b, h, p):
            looped = not isinstance(p, int)
            if h == 0 and isinstance(b, int) and b == 0:
                return (b, p + 1) if looped or p < PAIRS - 1 else None
            if h == 0:
                return (b, p + E_LATE) if looped or p == LOOP0 - 1 else None
            if h == H - 1 and (not isinstance(b, int) or b < FULL):
                return (b + 1, p - LOOP0) if looped else None
            return None

        def blocks(eng, body, first=0):
            for b in range(first):
                body(b)
            with eng.Fori(first, FULL - 1) as b:
                body(b)
            body(FULL - 1)
            body(FULL)

        with nc.Block() as block:
            @block.sync
            def _(sp):
                def store(b):
                    sp.wait_ge(o_out, (b + 1) * H * IT + 2 if not isinstance(b, int) or b < FULL
                               else FULL * H * IT + H * LASTW // P + 2)
                    if isinstance(b, int) and b == FULL:
                        r0 = FULL * BW
                        sp.dma_start(out[r0:r0 + P, :], out_acc[:, 0]).then_inc(out_st, 16)
                        sp.dma_start(out[r0 + P:N, :], out_acc[0:LASTP, 1]).then_inc(out_st, 16)
                    else:
                        sp.dma_start(out[bass.ds(b * BW, BW), :].rearrange("(t p) d -> p t d", p=P),
                                     out_acc[:, 0:IT]).then_inc(out_st, 16)

                def body(b):
                    if not isinstance(b, int) or b < FULL:
                        nxt = b + 1
                        for h in range(H - 1):
                            sp.wait_ge(p_ready, (b * H + h + 1) * PAIRS)
                            load_u(sp, nxt, h)
                        sp.wait_ge(e_sub, (b + 1) * NT)
                        load_max(sp, nxt)

                        for p in range(PAIRS):
                            sp.wait_ge(p_ready, (b * H + H - 1) * PAIRS + p + 1)
                            load_e(sp, nxt, p)
                        sp.wait_ge(p_ready, (b + 1) * H * PAIRS)
                        load_u(sp, nxt, H - 1)
                    store(b)
                    if not isinstance(b, int) or b < FULL:
                        sp.wait_ge(out_st, (b + 1) * 16)
                        load_x1(sp, nxt)
                    else:
                        sp.wait_ge(out_st, (FULL + 2) * 16)

                blocks(sp, body)

            @block.gpsimd
            def _(pool):
                def pairs_here(b, p0, p1):
                    for p in range(p0, p1):
                        pool.wait_ge(e_in[p], (b + 1) * 16)
                        pool.wait_ge(mb_in, (b + 1) * 16)
                        nc.gpsimd.tensor_tensor(ticks[:, p:p + 1], ones32[:], ones32[:], ALU.add).then_inc(e_here, 1)

                def add_halves(b, h):
                    W = width(b)
                    pool.wait_ge(acc_done, (b * H + h + 1) * PAIRS + T_RING)
                    nc.gpsimd.tensor_tensor(p_acc[:, h % 2, 0, 0:W], p_acc[:, h % 2, 0, 0:W], p_acc[:, h % 2, 1, 0:W],
                                            ALU.add).then_inc(acc_sum, 1)

                pairs_here(0, 0, PAIRS)

                def body(b):
                    for h in range(H - 1):
                        add_halves(b, h)
                    more = not isinstance(b, int) or b < FULL
                    if more:
                        pairs_here(b + 1, 0, LOOP1 - LOOP0)
                    add_halves(b, H - 1)
                    if more:
                        pairs_here(b + 1, LOOP1 - LOOP0, PAIRS)

                blocks(pool, body)

            @block.scalar
            def _(act):
                def exp_e(b, p):
                    W = width(b)
                    act.wait_ge(e_sub, b * NT + p * 2 + 2)
                    e = e_blk[:, bass.ds(p * 2, 2), 0:W]
                    nc.scalar.activation(e, e, ACT.Exp).then_inc(e_ready, 1)

                def t1(b, h, p):
                    W = width(b)
                    g = (b * H + h) * PAIRS + p
                    if isinstance(p, int) and p == 0:
                        act.wait_ge(u_in[h], (b + 1) * 16)
                    act.wait_ge(acc_done, g + 1)
                    for u in range(2):
                        nc.scalar.activation(t_ring[:, g % T_RING, u, 0:W], u_bc[:, h, 0, 0:W], ACT.Copy,
                                             scale=vv4[:, 0, h, bass.ds(p * 2 + u, 1)]).then_inc(t1_ready, 1)

                def step(b, h, p, after=None):
                    W = width(b)
                    g = (b * H + h) * PAIRS + p
                    after = after or ((b, h, p + 1) if not isinstance(p, int) or p < PAIRS - 1 else None)
                    if after:
                        t1(*after)
                    if e_of(b, h, p):
                        exp_e(*e_of(b, h, p))
                    act.wait_ge(hl_free, g + 1)
                    act.wait_ge(p_ready, g + 1)
                    nc.scalar.activation(hl_ring[:, g % HL_RING, 0, :, 0:W], t_ring[:, g % T_RING, :, 0:W],
                                         ACT.Copy).then_inc(hi_ready, 1)

                def evacuate(b, h):
                    W = width(b)
                    q = b * H + h
                    act.wait_ge(o_done, o_before(b, h) + 1)
                    for k in range(KT):
                        if k < KT - 1:
                            act.wait_ge(z_bank, q * (KT - 1) + k + 1)
                        else:
                            act.wait_ge(hl_free, (q + 1) * PAIRS + HL_RING)
                        nc.scalar.activation(z16[:, 0, k, 0:W], z_ps[:, k, 0:W], ACT.Copy,
                                             scale=ZS).then_inc(z_hi, 1)

                def segment(b, h):
                    nxt = seg_next(b, h)
                    for p in range(2, LOOP0):
                        step(b, h, p)
                    with act.Fori(LOOP0, LOOP1) as p:
                        step(b, h, p)
                    for p in range(LOOP1, PAIRS - 1):
                        step(b, h, p)
                    step(b, h, PAIRS - 1, after=nxt and (*nxt, 0))
                    if nxt:
                        for p in range(2):
                            step(*nxt, p)
                    evacuate(b, h)

                t1(0, 0, 0)
                exp_e(0, 0)
                for p in range(2):
                    step(0, 0, p)

                def body(b):
                    for h in range(H):
                        segment(b, h)

                blocks(act, body, first=1)

            @block.vector
            def _(dve):
                nc.vector.memset(credits[:, 6:7], 0.0).then_inc(acc_done, T_RING)
                nc.vector.memset(credits[:, 7:8], 0.0).then_inc(hl_free, HL_RING)
                nc.vector.memset(credits[:, 8:9], 0.0).then_inc(rs_ps, 2)
                nc.vector.memset(credits[:, 9:10], 0.0).then_inc(rs_sb, 1)
                nc.vector.memset(credits[:, 10:11], 0.0).then_inc(o_done, 1)
                nc.vector.memset(credits[:, 11:12], 0.0).then_inc(o_out, 2)

                def lo_part(b, h, p):
                    W = width(b)
                    g = (b * H + h) * PAIRS + p
                    dve.wait_ge(hi_ready, g + 1)
                    nc.vector.tensor_tensor(hl_ring[:, g % HL_RING, 1, :, 0:W], t_ring[:, g % T_RING, :, 0:W],
                                            hl_ring[:, g % HL_RING, 0, :, 0:W], ALU.subtract).then_inc(lo_ready, 1)

                def accumulate(b, h, p):
                    W = width(b)
                    q = b * H + h
                    g = q * PAIRS + p
                    tp = t_ring[:, g % T_RING, :, 0:W]
                    acc = p_acc[:, h % 2, :, 0:W]
                    if isinstance(p, int) and p == 0:
                        dve.wait_ge(rs_ps, q + 1)
                        nc.vector.tensor_scalar(acc, tp, 1.0, None, ALU.mult).then_inc(acc_done, 1)
                    else:
                        dve.wait_ge(acc_done, g + T_RING)
                        nc.vector.tensor_tensor(acc, acc, tp, ALU.add).then_inc(acc_done, 1)

                def subtract_max(b, p):
                    W = width(b)
                    dve.wait_ge(e_here, b * PAIRS + p + 1)
                    for u in range(2):
                        e = e_blk[:, p * 2 + u, 0:W]
                        nc.vector.tensor_tensor(e, e, max_bc[:, 0:W], ALU.subtract).then_inc(e_sub, 1)

                def step(b, h, p, before=None):
                    W = width(b)
                    g = (b * H + h) * PAIRS + p
                    before = before or ((b, h, p - 1) if not isinstance(p, int) or p > 0 else None)
                    tp = t_ring[:, g % T_RING, :, 0:W]
                    for u in range(2):
                        dve.wait_ge(t1_ready, g * 2 + u + 1)
                        tu = t_ring[:, g % T_RING, u, 0:W]
                        nc.vector.scalar_tensor_tensor(out=tu, in0=u_bc[:, h, 1, 0:W],
                                                       scalar=vv4[:, 1, h, bass.ds(p * 2 + u, 1)], in1=tu,
                                                       op0=ALU.mult, op1=ALU.max).then_inc(stt_done, 1)
                    if before:
                        lo_part(*before)
                    if e_of(b, h, p):
                        subtract_max(*e_of(b, h, p))
                    dve.wait_ge(stt_done, g * 2 + 2)
                    if h == 0:
                        dve.wait_ge(e_ready, b * PAIRS + p + 1)
                    nc.vector.tensor_tensor(tp, tp, e_blk[:, bass.ds(p * 2, 2), 0:W], ALU.mult).then_inc(p_ready, 1)
                    if before:
                        accumulate(*before)

                def evacuate_z(b, h):
                    W = width(b)
                    q = b * H + h
                    for k in range(KT):
                        dve.wait_ge(z_hi, q * KT + k + 1)
                        nc.vector.scalar_tensor_tensor(out=z16[:, 1, k, 0:W], in0=z_ps[:, k, 0:W], scalar=ZS,
                                                       in1=z16[:, 0, k, 0:W], op0=ALU.mult,
                                                       op1=ALU.subtract).then_inc(z_lo, 1)

                def row_factors(b, h):
                    q = b * H + h
                    n = width(b) // P
                    dve.wait_ge(rs_ps, q + 3)
                    nc.vector.reciprocal(rinv[:, 0:n], c_ps[:, 0:n]).then_inc(rinv_done, 1)
                    dve.wait_ge(rinv_done, q + 1)
                    nc.vector.tensor_scalar(rcoef[:, 0:n], rinv[:, 0:n], coef0[:], None,
                                            ALU.mult).then_inc(rs_sb, 1)
                    dve.wait_ge(rs_sb, q + 2)
                    if h == 0:
                        dve.wait_ge(x1_in, (b + 1) * 16)

                def add_out(b, h, its):
                    n = width(b) // P
                    for it in its:
                        f = o_before(b, h) + it
                        dve.wait_ge(o_done, f + 2)
                        if h > 0:
                            dve.wait_ge(o_out, f - n + 3)
                        nc.vector.scalar_tensor_tensor(out=out_acc[:, it], in0=o_ps[:, it % 3],
                                                       scalar=rcoef[:, it:it + 1], in1=out_acc[:, it],
                                                       op0=ALU.mult, op1=ALU.add).then_inc(o_out, 1)

                def segment(b, h):
                    for p in range(4, LOOP0):
                        step(b, h, p)
                    with dve.Fori(LOOP0, LOOP1) as p:
                        step(b, h, p)
                    for p in range(LOOP1, PAIRS):
                        step(b, h, p)
                    last = (b, h, PAIRS - 1)
                    nxt = seg_next(b, h)
                    if nxt:
                        step(*nxt, 0, before=last)
                        step(*nxt, 1)
                    else:
                        lo_part(*last)
                        dve.wait_ge(p_ready, (b * H + H) * PAIRS)
                        accumulate(*last)
                    evacuate_z(b, h)
                    if nxt:
                        step(*nxt, 2)
                    row_factors(b, h)
                    add_out(b, h, [0])
                    if nxt:
                        step(*nxt, 3)
                    add_out(b, h, range(1, width(b) // P))

                subtract_max(0, 0)
                for p in range(4):
                    step(0, 0, p)

                def body(b):
                    for h in range(H):
                        segment(b, h)

                blocks(dve, body, first=1)

            @block.tensor
            def _(pe):
                def pair(b, h, p, first=False, last=False, before=None):
                    W = width(b)
                    g = (b * H + h) * PAIRS + p
                    r = g % HL_RING
                    pe.wait_ge(lo_ready, g + 1)
                    for k in range(KT):
                        if before is not None:
                            pe.wait_ge(z_lo, before * KT + k + 1)
                        for u in range(2):
                            hk = [h16[:, s, p * 2 + u, k * P:(k + 1) * P] for s in range(2)]
                            for n, (hs, ps) in enumerate(((0, 0), (0, 1), (1, 0))):
                                mm = nc.tensor.matmul(z_ps[:, k, 0:W], hk[hs], hl_ring[:, r, ps, u, 0:W],
                                                      start=first and u == 0 and n == 0,
                                                      stop=last and u == 1 and n == 2)
                        if k == KT - 1:
                            mm.then_inc(hl_free, 1)
                        elif last:
                            mm.then_inc(z_bank, 1)

                def project(b, h):
                    W = width(b)
                    n = W // P
                    q = b * H + h
                    pe.wait_ge(acc_sum, q + 1)
                    pe.wait_ge(rs_sb, q + 1)
                    for it in range(n):
                        mm = nc.tensor.matmul(c_ps[:, it:it + 1], p_acc[:, h % 2, 0, it * P:(it + 1) * P],
                                              ones32[:], start=True, stop=True)
                    mm.then_inc(rs_ps, 1)
                    pe.wait_ge(z_lo, (q + 1) * KT)
                    for it in range(n):
                        pe.wait_ge(o_out, o_before(b, h) + 2 + (it >= 3))
                        for k in range(KT):
                            for m, (zs, ws) in enumerate(((0, 0), (0, 1), (1, 0))):
                                mm = nc.tensor.matmul(o_ps[:, it % 3], z16[:, zs, k, it * P:(it + 1) * P],
                                                      w16[:, k, h, ws], start=k == 0 and m == 0,
                                                      stop=k == KT - 1 and m == 2)
                        mm.then_inc(o_done, 1)

                def segment(b, h):
                    if isinstance(b, int) and b == FULL:
                        for p in range(1, PAIRS - 1):
                            pair(b, h, p)
                    else:
                        with pe.Fori(1, PAIRS - 1) as p:
                            pair(b, h, p)
                    pair(b, h, PAIRS - 1, last=True)
                    nxt = seg_next(b, h)
                    if nxt:
                        pair(*nxt, 0, first=True, before=b * H + h)
                    project(b, h)

                pair(0, 0, 0, first=True)

                def body(b):
                    for h in range(H):
                        segment(b, h)

                blocks(pe, body)


def kernel(x, adj, L0_gnn_W, L0_gnn_b, L1_gnn_W, L1_gnn_a):
    import numpy as np
    import concourse.bacc as bacc
    from concourse.bass_utils import run_bass_kernel_spmd

    x, adj = np.asarray(x), np.asarray(adj)
    adjT = adj.T
    adjT = np.concatenate([adjT, adjT[:, N - 1:]], axis=1)
    adjT = np.ascontiguousarray(np.concatenate([adjT, adjT[N - 1:]], axis=0))
    arrays = {
        "x_in": np.ascontiguousarray(np.concatenate([x, x[N - 1:]], axis=0)),
        "adjT_in": adjT,
        "W0_in": np.ascontiguousarray(L0_gnn_W),
        "b0_in": np.ascontiguousarray(L0_gnn_b),
        "W1_in": np.ascontiguousarray(L1_gnn_W),
        "a1_in": np.ascontiguousarray(L1_gnn_a),
    }
    nc = bacc.Bacc("TRN2", target_bir_lowering=False, num_devices=1)
    args = [nc.dram_tensor(name, a.shape, mybir.dt.from_np(a.dtype), kind="ExternalInput").ap()
            for name, a in arrays.items()]
    out = nc.dram_tensor("out_dram", (N, D), F32, kind="ExternalOutput").ap()
    gnn_kernel(nc, *args, out)
    result = run_bass_kernel_spmd(nc, [arrays], core_ids=[0])
    return result.results[0]["out_dram"]
```
